# Optimizing a Trainium2 kernel written in Bass

```python
import numpy as np
import jax
import jax.numpy as jnp

def _softmax(x, axis=-1):
    return jax.nn.softmax(x, axis=axis)

def _gelu(x):
    return jax.nn.gelu(x, approximate=True)

def _silu(x):
    return jax.nn.silu(x)

def _sigmoid(x):
    return jax.nn.sigmoid(x)

def _layernorm(x, axis=-1, eps=1e-05):
    m = jnp.mean(x, axis=axis, keepdims=True)
    v = jnp.var(x, axis=axis, keepdims=True)
    return (x - m) / jnp.sqrt(v + eps)

def _scatter_add(tgt, idx, src, axis=0):
    return tgt.at[idx].add(src)

def _segment_sum(src, seg, n):
    return jax.ops.segment_sum(src, seg, n)
kernel_name = 'mk_gnn_preln_d2_gnn_r8_48a6f7'

def setup_inputs(seed: int=0):
    np.random.seed(seed)
    _w = jnp.asarray

    def _rec_inputs():
        import jax
        import jax.numpy as jnp
        _gk = jax.random.key(seed)
        x = -0.0005121 + 1.001 * jax.random.normal(jax.random.fold_in(_gk, 1), (12500, 32), jnp.float32)
        src = jax.random.randint(jax.random.fold_in(_gk, 2), (400000,), 0, 12500, jnp.int32)
        dst = jax.random.randint(jax.random.fold_in(_gk, 3), (400000,), 0, 12500, jnp.int32)
        _o = jnp.argsort(dst, stable=True)
        src = src[_o]
        dst = dst[_o]
        edge_type_86 = jax.random.randint(jax.random.fold_in(_gk, 12), (400000,), 0, 86, jnp.int32)
        node_vec1 = jax.random.uniform(jax.random.fold_in(_gk, 13), (12500, 1), jnp.float32, 0.0, 0.999991)
        node_vec1_n2 = jax.random.uniform(jax.random.fold_in(_gk, 14), (12500, 1), jnp.float32, 0.0, 0.999991)
        return (x, src, dst, edge_type_86, node_vec1, node_vec1_n2)
    x, src, dst, edge_type_86, node_vec1, node_vec1_n2 = _rec_inputs()

    def _L0_gnn_setup():
        import jax, jax.numpy as jnp
        import numpy as np
        N_NODES = 12500
        N_EDGES = 200000
        D_FEAT = 32
        key = jax.random.key(seed)
        k1, k2, k3, k4, k5 = jax.random.split(key, 5)
        src_feats = jax.random.normal(k1, (N_NODES, D_FEAT), dtype=jnp.float32)
        cj = jax.random.uniform(k2, (N_NODES, 1), dtype=jnp.float32)
        ci = jax.random.uniform(k3, (N_NODES, 1), dtype=jnp.float32)
        src_idx = jax.random.randint(k4, (N_EDGES,), 0, N_NODES, dtype=jnp.int32)
        dst_idx = jax.random.randint(k5, (N_EDGES,), 0, N_NODES, dtype=jnp.int32)
        return {'src_feats': src_feats, 'cj': cj, 'ci': ci, 'src_idx': src_idx, 'dst_idx': dst_idx}
    _L0_gnn_all = _L0_gnn_setup()
    _L0_gnn_in = {k: v for k, v in _L0_gnn_all.items() if k in ()}
    del _L0_gnn_all

    def _L1_gnn_setup():
        import jax, jax.numpy as jnp
        import numpy as np
        N_NODES = 6250
        N_EDGES = 100000
        INP_DIM = 32
        OUT_DIM = 32
        ATTN_DIM = 32
        NUM_RELS = 86
        NUM_BASES = 16
        GAMMA = 0.0
        key = jax.random.key(seed)
        ks = jax.random.split(key, 12)
        return {'h': jax.random.normal(ks[0], (N_NODES, INP_DIM), jnp.float32), 'weight': jax.random.normal(ks[1], (NUM_BASES, INP_DIM, OUT_DIM), jnp.float32), 'w_comp': jax.random.normal(ks[2], (NUM_RELS, NUM_BASES), jnp.float32), 'self_loop_weight': jax.random.normal(ks[3], (INP_DIM, OUT_DIM), jnp.float32), 'A1_w': jax.random.normal(ks[4], (ATTN_DIM, INP_DIM), jnp.float32), 'A1_b': jax.random.normal(ks[5], (ATTN_DIM,), jnp.float32), 'A2_w': jax.random.normal(ks[6], (ATTN_DIM, INP_DIM), jnp.float32), 'A2_b': jax.random.normal(ks[7], (ATTN_DIM,), jnp.float32), 'rel_emb': jax.random.normal(ks[8], (NUM_RELS, ATTN_DIM), jnp.float32), 'src': jax.random.randint(ks[9], (N_EDGES,), 0, N_NODES, jnp.int32), 'dst': jax.random.randint(ks[10], (N_EDGES,), 0, N_NODES, jnp.int32), 'etype': jax.random.randint(ks[11], (N_EDGES,), 0, NUM_RELS, jnp.int32)}
    _L1_gnn_all = _L1_gnn_setup()
    _L1_gnn_in = {k: v for k, v in _L1_gnn_all.items() if k in ('weight', 'w_comp', 'self_loop_weight', 'A1_w', 'A1_b', 'A2_w', 'A2_b', 'rel_emb')}
    del _L1_gnn_all
    return {'x': x, 'src': src, 'dst': dst, 'edge_type_86': edge_type_86, 'node_vec1': node_vec1, 'node_vec1_n2': node_vec1_n2, 'L1_gnn_weight': _L1_gnn_in['weight'], 'L1_gnn_w_comp': _L1_gnn_in['w_comp'], 'L1_gnn_self_loop_weight': _L1_gnn_in['self_loop_weight'], 'L1_gnn_A1_w': _L1_gnn_in['A1_w'], 'L1_gnn_A1_b': _L1_gnn_in['A1_b'], 'L1_gnn_A2_w': _L1_gnn_in['A2_w'], 'L1_gnn_A2_b': _L1_gnn_in['A2_b'], 'L1_gnn_rel_emb': _L1_gnn_in['rel_emb']}

def reference(x, src, dst, edge_type_86, node_vec1, node_vec1_n2, L1_gnn_weight, L1_gnn_w_comp, L1_gnn_self_loop_weight, L1_gnn_A1_w, L1_gnn_A1_b, L1_gnn_A2_w, L1_gnn_A2_b, L1_gnn_rel_emb):
    import jax
    import jax.numpy as jnp

    def _L0_gnn_ref(src_feats, cj, ci, src_idx, dst_idx):
        import jax, jax.numpy as jnp
        import numpy as np
        N_NODES = 12500
        N_EDGES = 200000
        D_FEAT = 32
        weighted = src_feats * cj
        msgs = weighted[src_idx]
        agg = jax.ops.segment_sum(msgs, dst_idx, num_segments=N_NODES)
        return agg * ci

    def _L1_gnn_ref(h, weight, w_comp, self_loop_weight, A1_w, A1_b, A2_w, A2_b, rel_emb, src, dst, etype):
        import jax, jax.numpy as jnp
        import numpy as np
        N_NODES = 6250
        N_EDGES = 100000
        INP_DIM = 32
        OUT_DIM = 32
        ATTN_DIM = 32
        NUM_RELS = 86
        NUM_BASES = 16
        GAMMA = 0.0
        E = src.shape[0]
        N = h.shape[0]
        x = h[src]
        y = h[dst]
        c = w_comp[etype]
        xb = jnp.einsum('ei,bio->ebo', x, weight)
        msg = jnp.einsum('eb,ebo->eo', c, xb)
        x_hat = x @ A1_w.T + A1_b
        y_hat = y @ A2_w.T + A2_b + rel_emb[etype]
        scale = jnp.sqrt(jnp.asarray(INP_DIM, h.dtype))
        a = jnp.tanh(jax.nn.relu(jnp.sum(x_hat * y_hat, axis=-1) / scale))
        a = jnp.where(a > GAMMA, a, jnp.zeros_like(a))
        nei = jax.ops.segment_sum(a[:, None] * msg, dst, num_segments=N)
        last_e = jax.ops.segment_max(jnp.arange(E, dtype=jnp.int32), dst, num_segments=N)
        last_e = jnp.clip(last_e, 0, E - 1)
        curr = h[src[last_e]] @ self_loop_weight
        in_deg = jax.ops.segment_sum(jnp.ones((E,), h.dtype), dst, num_segments=N)
        h_new = jnp.where((in_deg > 0)[:, None], nei + curr, jnp.zeros_like(nei))
        return jax.nn.relu(h_new)
    h = jnp.maximum(_layernorm(x, axis=-1), 0.0)
    x = x + _L0_gnn_ref(h, node_vec1, node_vec1_n2, src, dst)
    h = jnp.maximum(_layernorm(x, axis=-1), 0.0)
    x = x + _L1_gnn_ref(h, L1_gnn_weight, L1_gnn_w_comp, L1_gnn_self_loop_weight, L1_gnn_A1_w, L1_gnn_A1_b, L1_gnn_A2_w, L1_gnn_A2_b, L1_gnn_rel_emb, src, dst, edge_type_86)
    return x

_drawn_inputs = setup_inputs


def setup_inputs(seed=0):
    import zlib

    import numpy as np

    out = dict(_drawn_inputs(seed))
    spreads = {}
    factors = {}
    for name, (base, spread) in spreads.items():
        noise = np.random.default_rng([zlib.crc32(name.encode()), seed]).standard_normal(out[name].shape)
        drawn = base * np.exp(spread * noise) if base else spread * noise
        out[name] = jnp.asarray(drawn.astype(out[name].dtype))
    for name, factor in factors.items():
        out[name] = (out[name] * factor).astype(out[name].dtype)
    return out
```

```python
import concourse.bass as bass
from concourse import mybir
from contextlib import ExitStack



def gnn_kernel(nc, x, src, dst, etype, cj, ci, weight, w_comp, w_self, a1_w, a1_b, a2_w, a2_b, rel_emb, out):
    f32 = mybir.dt.float32
    bf16 = mybir.dt.bfloat16
    i32 = mybir.dt.int32
    ALU = mybir.AluOpType
    ACT = mybir.ActivationFunctionType
    AX = mybir.AxisListType.X

    N, D = x.shape
    E = src.shape[0]
    R, NB = w_comp.shape
    GROUPS = 125
    GE = E // GROUPS
    CH = GE // 128
    UNITS = 5
    UC = CH // UNITS
    UE = UC * 128
    WIN = 128
    TILES = -(-N // WIN)
    PN = 125
    NT = N // PN
    NPAD = N + WIN
    BIG = 1.0e6
    EPS = 1e-5
    YC = D + NB + 1
    F0 = 3 * D
    OB = D * NB
    QB = OB // 128
    assert E == GROUPS * GE and GE == 128 * CH and CH == UNITS * UC and N == PN * NT and OB == 512

    table0 = nc.dram_tensor("table0", [N, F0], bf16).ap()
    table1 = nc.dram_tensor("table1", [N, 2 * D], f32).ap()
    dst_table = nc.dram_tensor("dst_table", [NPAD, 3 * YC], bf16).ap()
    keys = nc.dram_tensor("keys", [2 * GROUPS, GE], f32).ap()
    key_rows = nc.dram_tensor("key_rows", [GROUPS, GE], bf16).ap()
    type_rows = nc.dram_tensor("type_rows", [GROUPS, GE], bf16).ap()

    ctx = ExitStack()
    with ctx:
        def sb(name, shape, dt):
            return ctx.enter_context(nc.sbuf_tensor(name, shape, dt))

        acc = sb("acc", [128, NPAD], f32)
        xb = sb("xb", [PN, NT, D], f32)
        srcT = sb("srcT", [128, GROUPS + 1, CH], i32)
        keyT = sb("keyT", [128, GROUPS, CH], f32)
        local_e = sb("local_e", [128, GE], f32)
        ident = sb("ident", [128, 128], f32)
        iota_r = sb("iota_r", [128, 128], f32)
        iota_p = sb("iota_p", [128, 1], f32)
        edge_no = sb("edge_no", [128, CH], f32)
        off = sb("off", [128, 1], f32)
        off_next = sb("off_next", [128, 1], f32)
        base_col = sb("base_col", [128, 1], f32)
        max_col = sb("max_col", [128, 1], f32)
        base0 = sb("base0", [1, GROUPS], f32)
        base_f = sb("base_f", [1, GROUPS + 1], f32)
        base_i = sb("base_i", [1, GROUPS + 1], i32)
        passes_f = sb("passes_f", [1, 1], f32)
        passes_i = sb("passes_i", [1, 1], i32)
        cjt = sb("cjt", [PN, NT], f32)
        cit = sb("cit", [PN, NT], f32)
        mean = sb("mean", [PN, NT], f32)
        var = sb("var", [PN, NT], f32)
        std = sb("std", [PN, NT], f32)
        sum_w = sb("sum_w", [128, D + 1], f32)
        both_a = sb("both_a", [128, 4, 2 * D], f32)
        b1_row = sb("b1_row", [128, D], f32)
        b2_row = sb("b2_row", [128, D], f32)
        w_flat = sb("w_flat", [128, QB, D], f32)
        w_selft = sb("w_selft", [D, D], f32)
        type_tab = sb("type_tab", [R, YC], f32)
        type_left = sb("type_left", [R, YC], f32)
        type_tabs = sb("type_tabs", [R, 3, YC], bf16)
        group_ofs = sb("group_ofs", [128, 1], f32)
        banks = [ctx.enter_context(nc.psum_tensor(f"bank{i}", [128, 512], f32)) for i in range(8)]

        def sem(name):
            return nc.alloc_semaphore(name)

        loaded = {n: sem(f"loaded_{n}") for n in
                  ("dst", "src", "type", "x", "cj", "ci", "small", "sums", "blocks")}
        stored = sem("stored")
        stored_pad = sem("stored_pad")
        stored_out = sem("stored_out")
        iota_done = sem("iota_done")
        consts_done = sem("consts_done")
        prep_chain = sem("prep_chain")
        keys_done = sem("keys_done")
        types_done = sem("types_done")
        src_f_done = sem("src_f_done")
        cols_done = sem("cols_done")
        cols_turned = sem("cols_turned")
        src_turned = sem("src_turned")
        src_copied = sem("src_copied")
        ln_chain = sem("ln_chain")
        ln_var = sem("ln_var")
        ln_std = sem("ln_std")
        table0_done = sem("table0_done")
        agg_made = sem("agg_made")
        agg_taken = sem("agg_taken")
        mid_chain = sem("mid_chain")
        h_done = sem("h_done")
        h_turned = sem("h_turned")
        h_copied = sem("h_copied")
        a_made = sem("a_made")
        a_taken = sem("a_taken")
        tables_done = sem("tables_done")
        last_turned = sem("last_turned")
        last_taken = sem("last_taken")
        last_chain = sem("last_chain")
        restart = sem("restart")

        keys_in = sem("keys_in")
        key_chain = sem("key_chain")
        key_rounded = sem("key_rounded")
        key_rows_out = sem("key_rows_out")
        keys_turned = sem("keys_turned")
        keys_copied = sem("keys_copied")
        idx_ready = sem("idx_ready")
        slot_free = sem("slot_free")
        pool_turn = sem("pool_turn")
        rows_free = sem("rows_free")
        hot_ready = sem("hot_ready")
        dve_chain = sem("dve_chain")
        last_ready = sem("last_ready")
        sums_ready = sem("sums_ready")
        sums_free = sem("sums_free")
        y_ready = sem("y_ready")
        y_free = sem("y_free")
        score_ready = sem("score_ready")
        att_ready = sem("att_ready")
        outer_ready = sem("outer_ready")
        outer_free = sem("outer_free")
        win_free = sem("win_free")
        g_copied = sem("g_copied")
        gt_ready = sem("gt_ready")
        gt_copied = sem("gt_copied")
        next_pass = sem("next_pass")
        acc_added = sem("acc_added")
        win_in = sem("win_in")
        key_in = [sem(f"key_in{u}") for u in range(UNITS)]
        type_in = [sem(f"type_in{u}") for u in range(UNITS)]
        gathered = [sem(f"gathered{u}") for u in range(UNITS)]
        of_pass = range(keys_in.num, gathered[-1].num + 1)
        of_gathers = range(gathered[0].num, gathered[-1].num + 1)

        class Chain:

            def __init__(self, engine, s, start=0):
                self.engine, self.s, self.start, self.n = engine, s, start, 0

            def __call__(self, ins):
                ins.then_inc(self.s, 1)
                self.n += 1
                self.engine.wait_ge(self.s, self.start + self.n)

        def along(col, n):
            return col.unsqueeze(2).to_broadcast([col.shape[0], col.shape[1], n])

        with ExitStack() as stage:
            def tmp(name, shape, dt):
                return stage.enter_context(nc.sbuf_tensor(name, shape, dt))

            dst_i = tmp("dst_i", [GROUPS, GE], i32)
            src_i = tmp("src_i", [GROUPS, GE], i32)
            type_i = tmp("type_i", [GROUPS, GE], i32)
            dst_f = tmp("dst_f", [GROUPS, GE], f32)
            src_f = tmp("src_f", [GROUPS, GE], f32)
            key0 = tmp("key0", [GROUPS, GE], f32)
            key_left = tmp("key_left", [GROUPS, GE], f32)
            type_b = tmp("type_b", [GROUPS, GE], bf16)
            with nc.allow_non_contiguous_dma(reason="transposed 32 x 32 weights, once"), nc.Block() as block:
                @block.sync
                def _(sp):
                    sp.dma_start(dst_i[:, :], dst.rearrange("(g e) -> g e", e=GE)).then_inc(loaded["dst"], 16)
                    sp.dma_start(src_i[:, :], src.rearrange("(g e) -> g e", e=GE)).then_inc(loaded["src"], 16)
                    sp.dma_start(type_i[:, :], etype.rearrange("(g e) -> g e", e=GE)).then_inc(loaded["type"], 16)
                    sp.dma_start(xb[:, :, :], x.rearrange("(p t) d -> p t d", t=NT)).then_inc(loaded["x"], 16)
                    sp.dma_start(cjt[:, :], cj.rearrange("(p t) o -> p (t o)", t=NT)).then_inc(loaded["cj"], 16)
                    sp.dma_start(cit[:, :], ci.rearrange("(p t) o -> p (t o)", t=NT)).then_inc(loaded["ci"], 16)
                    sp.wait_ge(keys_done, 2)
                    sp.dma_start(keys[0:GROUPS, :], key0[:, :]).then_inc(stored, 16)
                    sp.dma_start(keys[GROUPS:2 * GROUPS, :], key_left[:, :]).then_inc(stored, 16)
                    sp.wait_ge(types_done, 1)
                    sp.dma_start(type_rows, type_b[:, :]).then_inc(stored, 16)
                    for n in ("src", "x", "cj", "ci"):
                        sp.wait_ge(loaded[n], 16)
                    sp.wait_ge(stored, 48)

                @block.scalar
                def _(act):
                    act.wait_ge(consts_done, 1)
                    small = [
                        (both_a[0:D, 0, 0:D], a1_w.rearrange("a i -> i a")),
                        (both_a[0:D, 0, D:2 * D], a2_w.rearrange("a i -> i a")),
                        (b1_row[:, :], a1_b.rearrange("(o a) -> o a", o=1).to_broadcast([128, D])),
                        (b2_row[:, :], a2_b.rearrange("(o a) -> o a", o=1).to_broadcast([128, D])),
                        (w_flat[:, :, :], weight.rearrange("b i o -> (b i) o").rearrange("(q r) o -> r q o", r=128)),
                        (w_selft[:, :], w_self),
                        (type_tab[:, 0:D], rel_emb),
                        (type_tab[:, D:D + NB], w_comp),
                    ]
                    for to, of in small:
                        act.dma_start(to, of).then_inc(loaded["small"], 16)
                    act.wait_ge(consts_done, 2)
                    for part in range(3):
                        act.dma_start(sum_w[part * D:(part + 1) * D, 0:D], ident[0:D, 0:D]).then_inc(loaded["sums"], 16)
                    act.dma_start(sum_w[F0:F0 + 1, D:D + 1], ident[0:1, 0:1]).then_inc(loaded["sums"], 16)
                    act.wait_ge(loaded["sums"], 64)
                    act.wait_ge(loaded["small"], 16 * len(small))
                    for q in range(1, 4):
                        act.dma_start(both_a[q * D:(q + 1) * D, q, :], both_a[0:D, 0, :]).then_inc(loaded["blocks"], 16)
                    act.wait_ge(loaded["blocks"], 48)

                @block.gpsimd
                def _(pool):
                    opt = dict(allow_small_or_imprecise_dtypes=True)
                    pool.iota(iota_r[:, :], [[1, 128]], base=0, channel_multiplier=0, **opt).then_inc(iota_done, 1)
                    pool.iota(iota_p[:, :], [[0, 1]], base=0, channel_multiplier=1, **opt).then_inc(iota_done, 1)
                    pool.iota(local_e[:, :], [[1, GE]], base=1, channel_multiplier=0, **opt).then_inc(iota_done, 1)
                    pool.iota(edge_no[:, :], [[128, CH]], base=1, channel_multiplier=1, **opt).then_inc(iota_done, 1)
                    pool.memset(acc[:, :], 0.0).then_inc(iota_done, 1)
                    pool.wait_ge(iota_done, 5)

                @block.vector
                def _(dve):
                    link = Chain(dve, prep_chain)
                    for t in (sum_w, type_tab, off, off_next, base_f, group_ofs):
                        link(dve.memset(t[tuple([slice(None)] * len(t.shape))], 0.0))
                    link(dve.memset(both_a[:, :, :], 0.0))
                    dve.memset(srcT[:, GROUPS, :], 0).then_inc(consts_done, 1)
                    dve.wait_ge(iota_done, 5)
                    dve.tensor_scalar(ident[:, :], iota_r[:, :], iota_p[:, 0:1], None, ALU.is_equal)\
                       .then_inc(consts_done, 1)
                    dve.wait_ge(loaded["dst"], 16)
                    link(dve.tensor_copy(dst_f[:, :], dst_i[:, :]))
                    link(dve.tensor_reduce(base_col[0:GROUPS, :], dst_f[:, :], AX, ALU.min))
                    link(dve.tensor_scalar(key0[:, :], dst_f[:, :], base_col[0:GROUPS, 0:1], None, ALU.subtract))
                    dve.tensor_reduce(max_col[0:GROUPS, :], key0[:, :], AX, ALU.max).then_inc(cols_done, 1)
                    link(dve.tensor_scalar(key_left[:, :], key0[:, :], float(WIN), BIG, ALU.is_lt, ALU.mult))
                    dve.tensor_tensor(key_left[:, :], key_left[:, :], dst_f[:, :], ALU.add).then_inc(keys_done, 2)
                    dve.wait_ge(loaded["src"], 16)
                    dve.tensor_copy(src_f[:, :], src_i[:, :]).then_inc(src_f_done, 1)
                    dve.wait_ge(loaded["type"], 16)
                    dve.tensor_copy(type_b[:, :], type_i[:, :]).then_inc(types_done, 1)
                    dve.wait_ge(loaded["small"], 16 * 8)
                    link(dve.tensor_tensor(type_tab[:, 0:D], type_tab[:, 0:D], b2_row[0:R, :], ALU.add))
                    link(dve.tensor_copy(type_tabs[:, 0, :], type_tab[:, :]))
                    link(dve.tensor_tensor(type_left[:, :], type_tab[:, :], type_tabs[:, 0, :], ALU.subtract))
                    link(dve.tensor_copy(type_tabs[:, 1, :], type_left[:, :]))
                    link(dve.tensor_tensor(type_left[:, :], type_left[:, :], type_tabs[:, 1, :], ALU.subtract))
                    link(dve.tensor_copy(type_tabs[:, 2, :], type_left[:, :]))
                    dve.wait_ge(cols_turned, 2)
                    link(dve.tensor_copy(base0[:, :], banks[2][0:1, 0:GROUPS]))
                    link(dve.tensor_copy(base_f[:, 1:GROUPS + 1], base0[:, :]))
                    link(dve.tensor_copy(base_i[:, :], base_f[:, :]))
                    link(dve.tensor_reduce(passes_f[:, :], banks[2][0:1, 128:128 + GROUPS], AX, ALU.max))
                    link(dve.tensor_scalar(passes_f[:, :], passes_f[:, :], float(WIN), float(TILES), ALU.is_ge, ALU.mult))
                    link(dve.tensor_scalar(passes_f[:, :], passes_f[:, :], 1.0, None, ALU.add))
                    link(dve.tensor_copy(passes_i[:, :], passes_f[:, :]))
                    for b in range(0, CH, 4):
                        n = min(4, CH - b)
                        dve.wait_ge(src_turned, b // 4 + 1)
                        dve.tensor_copy(srcT[:, 0:GROUPS, b:b + n].rearrange("p g k -> p k g"),
                                        banks[b // 4 % 2][:, 0:n * GROUPS].rearrange("p (k g) -> p k g", g=GROUPS))\
                           .then_inc(src_copied, 1)

                @block.tensor
                def _(pe):
                    pe.wait_ge(consts_done, 2)
                    pe.wait_ge(cols_done, 1)
                    pe.transpose(banks[2][0:1, 0:GROUPS], base_col[0:GROUPS, :], ident[0:GROUPS, 0:GROUPS]).then_inc(cols_turned, 1)
                    pe.transpose(banks[2][0:1, 128:128 + GROUPS], max_col[0:GROUPS, :], ident[0:GROUPS, 0:GROUPS])\
                      .then_inc(cols_turned, 1)
                    pe.wait_ge(src_f_done, 1)
                    for b in range(0, CH, 4):
                        n = min(4, CH - b)
                        if b >= 8:
                            pe.wait_ge(src_copied, b // 4 - 1)
                        for k in range(n):
                            last = pe.transpose(banks[b // 4 % 2][:, k * GROUPS:(k + 1) * GROUPS],
                                                src_f[:, (b + k) * 128:(b + k + 1) * 128], ident[0:GROUPS, 0:GROUPS])
                        last.then_inc(src_turned, 1)

        def layer_norm(dve, link, to, of, scratch, vars_before):
            link(dve.tensor_reduce(mean[:, :], of, AX, ALU.add))
            link(dve.tensor_scalar(mean[:, :], mean[:, :], 1.0 / D, None, ALU.mult))
            link(dve.tensor_tensor(to, of, along(mean[:, :], D), ALU.subtract))
            link(dve.tensor_tensor(scratch, to, to, ALU.mult))
            link(dve.tensor_reduce(var[:, :], scratch, AX, ALU.add))
            dve.tensor_scalar(var[:, :], var[:, :], 1.0 / D, EPS, ALU.mult, ALU.add).then_inc(ln_var, 1)
            dve.wait_ge(ln_std, vars_before + 1)
            link(dve.reciprocal(std[:, :], std[:, :]))
            link(dve.tensor_tensor(to, to, along(std[:, :], D), ALU.mult))
            link(dve.tensor_scalar(to, to, 0.0, None, ALU.max))

        def take_root(act, n):
            act.wait_ge(ln_var, n)
            act.activation(std[:, :], var[:, :], ACT.Sqrt).then_inc(ln_std, 1)

        with ExitStack() as stage:
            h = stage.enter_context(nc.sbuf_tensor("h0", [PN, NT, D], f32))
            scratch = stage.enter_context(nc.sbuf_tensor("scratch0", [PN, NT, D], f32))
            parts = stage.enter_context(nc.sbuf_tensor("parts0", [PN, NT, 3, D], bf16))
            with nc.Block() as block:
                @block.scalar
                def _(act):
                    take_root(act, 1)

                @block.vector
                def _(dve):
                    link = Chain(dve, ln_chain)
                    layer_norm(dve, link, h[:, :, :], xb[:, :, :], scratch[:, :, :], 0)
                    link(dve.tensor_tensor(h[:, :, :], h[:, :, :], along(cjt[:, :], D), ALU.mult))
                    link(dve.tensor_copy(parts[:, :, 0, :], h[:, :, :]))
                    link(dve.tensor_tensor(h[:, :, :], h[:, :, :], parts[:, :, 0, :], ALU.subtract))
                    link(dve.tensor_copy(parts[:, :, 1, :], h[:, :, :]))
                    link(dve.tensor_tensor(h[:, :, :], h[:, :, :], parts[:, :, 1, :], ALU.subtract))
                    dve.tensor_copy(parts[:, :, 2, :], h[:, :, :]).then_inc(table0_done, 1)

                @block.sync
                def _(sp):
                    sp.wait_ge(table0_done, 1)
                    sp.dma_start(table0.rearrange("(p t) f -> p (t f)", t=NT),
                                 parts[:, :, :, :].rearrange("p t s d -> p (t s d)")).then_inc(stored, 16)
                    sp.wait_ge(stored, 64)

        def prepare_pass(p, tag):
            with ExitStack() as stage:
                key = stage.enter_context(nc.sbuf_tensor(f"pass_key{tag}", [GROUPS, GE], f32))
                key_b = stage.enter_context(nc.sbuf_tensor(f"pass_key_b{tag}", [GROUPS, GE], bf16))
                with nc.Block() as block:
                    @block.sync
                    def _(sp):
                        version = (p + 127) // 128 * GROUPS
                        sp.dma_start(key[:, :], keys[bass.ds(version, GROUPS), :]).then_inc(keys_in, 16)
                        sp.wait_ge(key_rounded, 1)
                        sp.dma_start(key_rows, key_b[:, :]).then_inc(key_rows_out, 16)
                        sp.wait_ge(key_rows_out, 16)

                    @block.vector
                    def _(dve):
                        dve.wait_ge(keys_in, 16)
                        dve.tensor_scalar(key[:, :], key[:, :], off[0:GROUPS, 0:1], None, ALU.subtract).then_inc(key_chain, 1)
                        dve.wait_ge(key_chain, 1)
                        dve.tensor_copy(key_b[:, :], key[:, :]).then_inc(key_rounded, 1)
                        dve.memset(group_ofs[:, :], 0.0).then_inc(key_chain, 1)
                        dve.wait_ge(key_chain, 2)

                    @block.tensor
                    def _(pe):
                        pe.wait_ge(key_chain, 1)
                        for b in range(0, CH, 4):
                            n = min(4, CH - b)
                            if b >= 8:
                                pe.wait_ge(keys_copied, b // 4 - 1)
                            for k in range(n):
                                last = pe.transpose(banks[b // 4 % 2][:, k * GROUPS:(k + 1) * GROUPS],
                                                    key[:, (b + k) * 128:(b + k + 1) * 128], ident[0:GROUPS, 0:GROUPS])
                            last.then_inc(keys_turned, 1)

                    @block.scalar
                    def _(act):
                        for b in range(0, CH, 4):
                            n = min(4, CH - b)
                            act.wait_ge(keys_turned, b // 4 + 1)
                            act.copy(keyT[:, :, b:b + n].rearrange("p g k -> p k g"),
                                     banks[b // 4 % 2][:, 0:n * GROUPS].rearrange("p (k g) -> p k g", g=GROUPS))\
                               .then_inc(keys_copied, 1)

        def close_pass():
            with nc.Block() as block:
                @block.vector
                def _(dve):
                    link = Chain(dve, next_pass)
                    link(dve.tensor_copy(off[:, :], off_next[:, :]))
                    link(dve.tensor_scalar(base_f[:, 1:GROUPS + 1], base_f[:, 1:GROUPS + 1], 0.0, off[0:1, 0:1], ALU.mult, ALU.add))
                    link(dve.tensor_copy(base_i[:, :], base_f[:, :]))
                    link(dve.tensor_scalar(off_next[:, :], off_next[:, :], float(WIN), None, ALU.add))
            nc.gpsimd.dma_reset(of_gathers)
            nc.all_engine_barrier(sems_to_clear=of_pass)

        def gather(pool, rows, idx, table):
            with pool.Fori(0, GROUPS) as g:
                for u in range(UNITS):
                    pool.wait_ge(idx_ready, UNITS * g + u + 1)
                    pool.wait_ge(slot_free, UNITS * g + u + 1)
                    pool.sem_inc(pool_turn, 1)
                    for k in range(UC):
                        pool.indirect_dma_start(rows[:, u, k, :], None, table,
                                                bass.IndirectOffsetOnAxis(ap=idx[:, u, k:k + 1], axis=0))\
                            .then_inc(gathered[u], 16)

        def window(eng, entry):
            return eng.value_load(base_i[0:1, bass.ds(entry, 1)], min_val=0, max_val=N - 1)

        passes = nc.values_load(passes_i[0:1, 0:1], min_val=1, max_val=TILES + 1)

        with nc.Fori(0, passes) as p:
            prepare_pass(p, 0)
            with ExitStack() as stage:
                def tmp(name, shape, dt):
                    return stage.enter_context(nc.sbuf_tensor(name, shape, dt))

                rows = tmp("rows0", [128, UNITS, UC, F0], bf16)
                idx = tmp("idx0", [128, UNITS, UC], i32)
                hot = tmp("hot0", [128, UNITS, UC, WIN], bf16)
                key_r = tmp("key_r0", [128, UNITS, UE], bf16)
                marked = tmp("marked", [128, UE], f32)
                unit_max = tmp("unit_max", [128, UNITS], f32)
                group_max = tmp("group_max", [128, 1], f32)
                group_last = tmp("group_last", [128, 1], f32)
                sums, lasts = banks[0], banks[1]
                with nc.Block() as block:
                    @block.gpsimd
                    def _(pool):
                        gather(pool, rows, idx, table0)

                    @block.sync
                    def _(sp):
                        with sp.Fori(0, GROUPS) as g:
                            for u in range(UNITS):
                                sp.wait_ge(rows_free, UNITS * g + u + 1)
                                sp.dma_start(key_r[:, u, :], key_rows[bass.ds(g, 1), u * UE:(u + 1) * UE].to_broadcast([128, UE]))\
                                  .then_inc(key_in[u], 16)

                    @block.vector
                    def _(dve):
                        dve.sem_inc(rows_free, UNITS)
                        dve.sem_inc(sums_free, 1)
                        for u in range(UNITS):
                            dve.tensor_copy(idx[:, u, :], srcT[:, 0, u * UC:(u + 1) * UC]).then_inc(idx_ready, 1)
                        steps = UNITS + 3
                        with dve.Fori(0, GROUPS) as g:
                            link = Chain(dve, dve_chain, steps * g)
                            for u in range(UNITS):
                                dve.wait_ge(slot_free, UNITS * g + u + 1)
                                dve.tensor_tensor(hot[:, u, :, :], along(keyT[:, bass.ds(g, 1), u * UC:(u + 1) * UC].squeeze(1), WIN),
                                                  iota_r[:, :].unsqueeze(1).to_broadcast([128, UC, WIN]), ALU.is_equal)\
                                   .then_inc(hot_ready, 1)
                                dve.wait_ge(key_in[u], 16 * g + 16)
                                dve.wait_ge(rows_free, UNITS * g + u + UNITS)
                                link(dve.scalar_tensor_tensor(marked[:, :], key_r[:, u, :], iota_p[:, 0:1],
                                                              local_e[:, u * UE:(u + 1) * UE], ALU.is_equal, ALU.mult))
                                dve.tensor_reduce(unit_max[:, u:u + 1], marked[:, :], AX, ALU.max).then_inc(rows_free, 1)
                                dve.wait_ge(gathered[u], 16 * UC * g + 16 * UC)
                                dve.tensor_copy(idx[:, u, :], srcT[:, bass.ds(g + 1, 1), u * UC:(u + 1) * UC].squeeze(1))\
                                   .then_inc(idx_ready, 1)
                            dve.wait_ge(rows_free, UNITS * g + 2 * UNITS)
                            link(dve.tensor_reduce(group_max[:, :], unit_max[:, :], AX, ALU.max))
                            link(dve.tensor_scalar(group_last[:, :], group_max[:, :], 0.0, group_ofs[:, 0:1], ALU.is_gt, ALU.mult))
                            dve.tensor_tensor(group_last[:, :], group_last[:, :], group_max[:, :], ALU.add).then_inc(last_ready, 1)
                            link(dve.tensor_scalar(group_ofs[:, :], group_ofs[:, :], float(GE), None, ALU.add))
                            at = window(dve, g + 1)
                            dve.wait_ge(sums_ready, g + 1)
                            dve.tensor_tensor(acc[0:F0, bass.ds(at, WIN)], acc[0:F0, bass.ds(at, WIN)], sums[0:F0, 0:WIN], ALU.add)\
                               .then_inc(acc_added, 1)
                            dve.tensor_tensor(acc[F0:F0 + 1, bass.ds(at, WIN)], acc[F0:F0 + 1, bass.ds(at, WIN)],
                                              lasts[F0:F0 + 1, 0:WIN], ALU.max).then_inc(sums_free, 1)
                            dve.wait_ge(sums_free, g + 2)
                            dve.wait_ge(acc_added, g + 1)

                    @block.tensor
                    def _(pe):
                        pe.sem_inc(slot_free, UNITS)
                        with pe.Fori(0, GROUPS) as g:
                            pe.wait_ge(sums_free, g + 1)
                            for u in range(UNITS):
                                pe.wait_ge(hot_ready, UNITS * g + u + 1)
                                pe.wait_ge(gathered[u], 16 * UC * g + 16 * UC)
                                for k in range(UC):
                                    last = pe.matmul(sums[0:F0, 0:WIN], rows[:, u, k, :], hot[:, u, k, :],
                                                     start=(u == 0 and k == 0), stop=(u == UNITS - 1 and k == UC - 1))
                                last.then_inc(slot_free, 1)
                            pe.wait_ge(last_ready, g + 1)
                            pe.matmul(lasts[F0:F0 + 1, 0:WIN], group_last[:, 0:1], ident[:, :], start=True, stop=True)\
                              .then_inc(sums_ready, 1)
            close_pass()

        with ExitStack() as stage:
            def tmp(name, shape, dt):
                return stage.enter_context(nc.sbuf_tensor(name, shape, dt))

            rows1 = tmp("rows1", [PN, NT, 2 * D], f32)
            row_y = tmp("row_y", [PN, NT, YC], f32)
            agg = tmp("agg", [PN, NT, D], f32)
            h_turned_sb = tmp("h_turned_sb", [128, 2, PN], f32)
            with nc.Block() as block:
                per = 15
                batches = [(b, min(per, NT - b)) for b in range(0, NT, per)]

                @block.tensor
                def _(pe):
                    for i, (b, n) in enumerate(batches):
                        if i >= 2:
                            pe.wait_ge(agg_taken, i - 1)
                        for t in range(n):
                            last = pe.matmul(banks[i % 2][0:PN, t * (D + 1):(t + 1) * (D + 1)],
                                             acc[0:F0 + 1, b + t:b + t + (PN - 1) * NT + 1:NT], sum_w[0:F0 + 1, :],
                                             start=True, stop=True)
                        last.then_inc(agg_made, 1)

                @block.vector
                def _(dve):
                    link = Chain(dve, mid_chain)
                    link(dve.memset(row_y[:, :, D:YC], 0.0))
                    for i, (b, n) in enumerate(batches):
                        dve.wait_ge(agg_made, i + 1)
                        made = banks[i % 2][0:PN, 0:n * (D + 1)].rearrange("p (t c) -> p t c", c=D + 1)
                        link(dve.tensor_tensor(agg[:, b:b + n, :], made[:, :, 0:D], along(cit[:, b:b + n], D), ALU.mult))
                        dve.tensor_copy(row_y[:, b:b + n, YC - 1:YC], made[:, :, D:D + 1]).then_inc(agg_taken, 1)
                    link(dve.tensor_tensor(xb[:, :, :], xb[:, :, :], agg[:, :, :], ALU.add))
                    layer_norm(dve, link, rows1[:, :, 0:D], xb[:, :, :], agg[:, :, :], 1)
                    link(dve.memset(off[:, :], 0.0))
                    link(dve.memset(off_next[:, :], 0.0))
                    link(dve.tensor_copy(base_f[:, 1:GROUPS + 1], base0[:, :]))
                    link(dve.tensor_copy(base_i[:, :], base_f[:, :]))
                    dve.wait_ge(agg_taken, len(batches))

                @block.scalar
                def _(act):
                    take_root(act, 2)

            with nc.Block() as block:
                quads = NT // 4

                @block.gpsimd
                def _(pool):
                    pool.memset(acc[0:D, :], 0.0).then_inc(restart, 1)
                    pool.wait_ge(restart, 1)

                @block.tensor
                def _(pe):
                    def turn(i):
                        if i >= 2:
                            pe.wait_ge(h_copied, i - 1)
                        pe.transpose(banks[i % 2][:, 0:PN], agg[:, 4 * i:4 * i + 4, :].rearrange("p t d -> p (t d)"),
                                     ident[0:PN, 0:PN]).then_inc(h_turned, 1)

                    pe.wait_ge(h_done, 1)
                    turn(0)
                    for i in range(quads):
                        if i + 1 < quads:
                            turn(i + 1)
                        pe.wait_ge(h_copied, i + 1)
                        if i >= 2:
                            pe.wait_ge(a_taken, 2 * i - 2)
                        pe.matmul(banks[2 + i % 2][0:PN, 0:8 * D], h_turned_sb[:, i % 2, :], both_a[:, :, :].rearrange("p q a -> p (q a)"),
                                  start=True, stop=True).then_inc(a_made, 1)

                @block.scalar
                def _(act):
                    for i in range(quads):
                        act.wait_ge(h_turned, i + 1)
                        if i >= 2:
                            act.wait_ge(a_made, i - 1)
                        act.copy(h_turned_sb[:, i % 2, :], banks[i % 2][:, 0:PN]).then_inc(h_copied, 1)

                @block.vector
                def _(dve):
                    dve.tensor_copy(agg[:, :, :], rows1[:, :, 0:D]).then_inc(h_done, 1)
                    for i in range(quads):
                        dve.wait_ge(a_made, i + 1)
                        made = banks[2 + i % 2][0:PN, 0:8 * D].rearrange("p (t c) -> p t c", c=2 * D)
                        dve.tensor_tensor(rows1[:, 4 * i:4 * i + 4, D:2 * D], made[:, :, 0:D],
                                          b1_row[0:PN, :].unsqueeze(1).to_broadcast([PN, 4, D]), ALU.add).then_inc(a_taken, 1)
                        dve.tensor_copy(row_y[:, 4 * i:4 * i + 4, 0:D], made[:, :, D:2 * D]).then_inc(a_taken, 1)
                    dve.wait_ge(a_taken, 2 * quads)

            parts = tmp("parts1", [PN, NT, 3, YC], bf16)
            zeros = tmp("zeros", [WIN, 3 * YC], bf16)
            with nc.Block() as block:
                @block.vector
                def _(dve):
                    link = Chain(dve, tables_done)
                    link(dve.memset(zeros[:, :], 0.0))
                    link(dve.tensor_copy(parts[:, :, 0, :], row_y[:, :, :]))
                    link(dve.tensor_tensor(row_y[:, :, :], row_y[:, :, :], parts[:, :, 0, :], ALU.subtract))
                    link(dve.tensor_copy(parts[:, :, 1, :], row_y[:, :, :]))
                    link(dve.tensor_tensor(row_y[:, :, :], row_y[:, :, :], parts[:, :, 1, :], ALU.subtract))
                    link(dve.tensor_copy(parts[:, :, 2, :], row_y[:, :, :]))

                @block.sync
                def _(sp):
                    sp.dma_start(table1.rearrange("(p t) f -> p (t f)", t=NT),
                                 rows1[:, :, :].rearrange("p t d -> p (t d)")).then_inc(stored, 16)
                    sp.wait_ge(tables_done, 6)
                    sp.dma_start(dst_table[0:N, :].rearrange("(p t) f -> p (t f)", t=NT),
                                 parts[:, :, :, :].rearrange("p t s d -> p (t s d)")).then_inc(stored, 16)
                    sp.dma_start(dst_table[N:NPAD, :], zeros[:, :]).then_inc(stored_pad, 16)
                    sp.wait_ge(stored, 96)
                    sp.wait_ge(stored_pad, 16)

        with nc.Fori(0, passes) as p:
            prepare_pass(p, 1)
            with ExitStack() as stage:
                def tmp(name, shape, dt):
                    return stage.enter_context(nc.sbuf_tensor(name, shape, dt))

                RING = 3
                rows = tmp("rows_in1", [128, UNITS, UC, 2 * D], f32)
                idx = tmp("idx1", [128, UNITS, UC], i32)
                key_r = tmp("key_r1", [128, UNITS, UE], bf16)
                type_r = tmp("type_r1", [R, UNITS, UE], bf16)
                node_hot = tmp("node_hot", [128, RING, UE], bf16)
                type_hot = tmp("type_hot", [R, RING, UE], bf16)
                hot = tmp("hot1", [128, RING, UC, WIN], f32)
                outer = tmp("outer", [128, RING, UC, OB], f32)
                last_h = tmp("last_h", [128, RING, UC, D], f32)
                prod = tmp("prod", [128, UC, D], f32)
                score = tmp("score", [128, 2, UC], f32)
                att = tmp("att", [128, 2, UC], f32)
                is_last = tmp("is_last", [128, UC], f32)
                att_c = tmp("att_c", [128, UC, NB], f32)
                edges_at = tmp("edges_at", [128, CH], f32)
                win_raw = tmp("win_raw", [128, 3, YC], bf16)
                win = tmp("win", [128, 3, YC], bf16)
                g_sb = tmp("g_sb", [128, OB + D], f32)
                gt_sb = tmp("gt_sb", [128, OB], f32)
                lt_sb = tmp("lt_sb", [D, 128], f32)
                y_banks, g_bank, l_bank, gt_bank, o_bank = banks[0:3], banks[3], banks[4], banks[5], banks[6]

                def before(u):
                    return {0: 2, 1: 2, 2: UNITS}.get(u, RING)

                assert UNITS == 5 and RING == 3
                with nc.Block() as block:
                    @block.gpsimd
                    def _(pool):
                        gather(pool, rows, idx, table1)

                    @block.sync
                    def _(sp):
                        with sp.Fori(0, GROUPS) as g:
                            at = window(sp, g + 1)
                            sp.wait_ge(win_free, g + 1)
                            sp.dma_start(win_raw[:, :, :], dst_table[bass.ds(at, WIN), :].rearrange("p (s c) -> p s c", c=YC))\
                              .then_inc(win_in, 16)
                            for u in range(UNITS):
                                sp.wait_ge(rows_free, 2 * UNITS * g + 2 * u + 2)
                                sp.dma_start(key_r[:, u, :], key_rows[bass.ds(g, 1), u * UE:(u + 1) * UE].to_broadcast([128, UE]))\
                                  .then_inc(key_in[u], 16)
                                sp.dma_start(type_r[:, u, :], type_rows[bass.ds(g, 1), u * UE:(u + 1) * UE].to_broadcast([R, UE]))\
                                  .then_inc(type_in[u], 16)

                    @block.scalar
                    def _(act):
                        act.sem_inc(win_free, 1)
                        act.sem_inc(g_copied, 2)
                        with act.Fori(0, GROUPS) as g:
                            act.wait_ge(win_in, 16 * g + 16)
                            act.wait_ge(y_ready, UNITS * g + UNITS)
                            act.copy(win[:, :, :], win_raw[:, :, :]).then_inc(win_free, 1)
                            for u in range(UNITS):
                                act.wait_ge(score_ready, UNITS * g + u + 1)
                                act.activation(att[:, u % 2, :], score[:, u % 2, :], ACT.Tanh, scale=float(D) ** -0.5)\
                                   .then_inc(att_ready, 1)
                                if u == 2:
                                    act.wait_ge(gt_ready, g + 1)
                                    act.copy(gt_sb[:, :], gt_bank[:, :])
                                    act.copy(lt_sb[:, :], o_bank[0:D, 0:128]).then_inc(gt_copied, 1)
                            act.wait_ge(outer_free, UNITS * g + 2 * UNITS)
                            act.copy(g_sb[:, 0:OB], g_bank[:, :]).then_inc(g_copied, 1)
                            act.copy(g_sb[:, OB:OB + D], l_bank[:, 0:D]).then_inc(g_copied, 1)
                        act.wait_ge(gt_ready, GROUPS + 1)
                        act.copy(gt_sb[:, :], gt_bank[:, :])
                        act.copy(lt_sb[:, :], o_bank[0:D, 0:128]).then_inc(gt_copied, 1)

                    @block.vector
                    def _(dve):
                        pre = Chain(dve, dve_chain)
                        pre(dve.memset(g_sb[:, :], 0.0))
                        pre(dve.tensor_copy(edges_at[:, :], edge_no[:, :]))
                        dve.sem_inc(rows_free, 2 * UNITS)
                        dve.sem_inc(slot_free, UNITS)
                        dve.sem_inc(y_free, UNITS)
                        dve.sem_inc(sums_free, 1)
                        for u in range(UNITS):
                            dve.tensor_copy(idx[:, u, :], srcT[:, 0, u * UC:(u + 1) * UC]).then_inc(idx_ready, 1)

                        def add_window(entry, n):
                            at = window(dve, entry)
                            dve.wait_ge(sums_ready, n)
                            dve.tensor_tensor(acc[0:D, bass.ds(at, WIN)], acc[0:D, bass.ds(at, WIN)], o_bank[0:D, 128:256], ALU.add)\
                               .then_inc(sums_free, 1)

                        with dve.Fori(0, GROUPS) as g:
                            link = Chain(dve, dve_chain, (UNITS * 4 + 1) * g + 2)

                            def hot_rows(u):
                                dve.wait_ge(y_ready, UNITS * g + u - before(u) + 1 + UNITS)
                                dve.wait_ge(key_in[u], 16 * g + 16)
                                dve.tensor_scalar(node_hot[:, u % RING, :], key_r[:, u, :], iota_p[:, 0:1], None, ALU.is_equal)\
                                   .then_inc(rows_free, 1)
                                dve.wait_ge(type_in[u], 16 * g + 16)
                                dve.tensor_scalar(type_hot[:, u % RING, :], type_r[:, u, :], iota_p[0:R, 0:1], None, ALU.is_equal)\
                                   .then_inc(rows_free, 1)

                            hot_rows(0)
                            for u in range(UNITS):
                                if u + 1 < UNITS:
                                    hot_rows(u + 1)
                                r, y = u % RING, y_banks[u % RING][:, 0:UC * YC].rearrange("p (k c) -> p k c", c=YC)
                                h_e = rows[:, u, :, 0:D]
                                dve.wait_ge(y_ready, UNITS * g + u + 1 + UNITS)
                                dve.wait_ge(gathered[u], 16 * UC * g + 16 * UC)
                                link(dve.tensor_tensor(prod[:, :, :], rows[:, u, :, D:2 * D], y[:, :, 0:D], ALU.mult))
                                link(dve.tensor_reduce(score[:, u % 2, :], prod[:, :, :], AX, ALU.add))
                                dve.tensor_scalar(score[:, u % 2, :], score[:, u % 2, :], 0.0, None, ALU.max).then_inc(score_ready, 1)
                                link(dve.tensor_tensor(is_last[:, :], y[:, :, YC - 1], edges_at[:, u * UC:(u + 1) * UC], ALU.is_equal))
                                dve.wait_ge(outer_free, UNITS * g + u - before(u) + 1 + UNITS)
                                dve.tensor_tensor(last_h[:, r, :, :], h_e, along(is_last[:, :], D), ALU.mult)
                                dve.tensor_tensor(hot[:, r, :, :], along(keyT[:, bass.ds(g, 1), u * UC:(u + 1) * UC].squeeze(1), WIN),
                                                  iota_r[:, :].unsqueeze(1).to_broadcast([128, UC, WIN]), ALU.is_equal)
                                dve.wait_ge(att_ready, UNITS * g + u + 1)
                                dve.tensor_tensor(att_c[:, :, :], y[:, :, D:D + NB], along(att[:, u % 2, :], NB), ALU.mult)\
                                   .then_inc(y_free, 1)
                                dve.wait_ge(y_free, UNITS * g + u + 1 + UNITS)
                                dve.tensor_tensor(outer[:, r, :, :].rearrange("p k (b i) -> p k b i", i=D),
                                                  att_c[:, :, :].unsqueeze(3).to_broadcast([128, UC, NB, D]),
                                                  h_e.unsqueeze(2).to_broadcast([128, UC, NB, D]), ALU.mult).then_inc(outer_ready, 1)
                                link(dve.tensor_copy(idx[:, u, :], srcT[:, bass.ds(g + 1, 1), u * UC:(u + 1) * UC].squeeze(1)))
                                dve.sem_inc(idx_ready, 1)
                                dve.sem_inc(slot_free, 1)
                                if u == 3:
                                    add_window(g, g + 1)
                            link(dve.tensor_scalar(edges_at[:, :], edges_at[:, :], float(GE), None, ALU.add))
                            dve.wait_ge(sums_free, g + 2)
                        add_window(GROUPS, GROUPS + 1)
                        dve.wait_ge(sums_free, GROUPS + 2)

                    @block.tensor
                    def _(pe):
                        pe.sem_inc(y_ready, UNITS)
                        pe.sem_inc(outer_free, UNITS)

                        def look_up(g, u):
                            pe.wait_ge(rows_free, 2 * UNITS * g + 2 * u + 2 + 2 * UNITS)
                            pe.wait_ge(y_free, UNITS * g + u - before(u) + 1 + UNITS)
                            for k in range(UC):
                                for n in range(6):
                                    if n < 3:
                                        left, right = node_hot[:, u % RING, k * 128:(k + 1) * 128], win[:, n, :]
                                    else:
                                        left, right = type_hot[:, u % RING, k * 128:(k + 1) * 128], type_tabs[:, n - 3, :]
                                    last = pe.matmul(y_banks[u % RING][:, k * YC:(k + 1) * YC], left, right,
                                                     start=(n == 0), stop=(n == 5))
                            last.then_inc(y_ready, 1)

                        def gather_sums(g, u):
                            pe.wait_ge(outer_ready, UNITS * g + u + 1)
                            if u == 0:
                                pe.wait_ge(g_copied, 2 * g + 2)
                            for k in range(UC):
                                first, end = u == 0 and k == 0, u == UNITS - 1 and k == UC - 1
                                pe.matmul(g_bank[:, :], hot[:, u % RING, k, :], outer[:, u % RING, k, :], start=first, stop=end)
                                last = pe.matmul(l_bank[:, 0:D], hot[:, u % RING, k, :], last_h[:, u % RING, k, :],
                                                 start=first, stop=end)
                            last.then_inc(outer_free, 1)

                        def turn_sums(n):
                            pe.wait_ge(g_copied, 2 * n)
                            for q in range(QB):
                                pe.transpose(gt_bank[:, q * 128:(q + 1) * 128], g_sb[:, q * 128:(q + 1) * 128], ident[:, :])
                            pe.wait_ge(sums_free, n)
                            pe.transpose(o_bank[0:D, 0:128], g_sb[:, OB:OB + D], ident[:, :]).then_inc(gt_ready, 1)

                        def weigh_sums(n):
                            pe.wait_ge(gt_copied, n)
                            for q in range(QB):
                                pe.matmul(o_bank[0:D, 128:256], w_flat[:, q, :], gt_sb[:, q * 128:(q + 1) * 128],
                                          start=(q == 0), stop=False)
                            pe.matmul(o_bank[0:D, 128:256], w_selft[:, :], lt_sb[:, :], start=False, stop=True).then_inc(sums_ready, 1)

                        with pe.Fori(0, GROUPS) as g:
                            pe.wait_ge(win_free, g + 2)
                            for u in range(UNITS):
                                look_up(g, u)
                                if u >= 1:
                                    gather_sums(g, u - 1)
                                if u == 1:
                                    turn_sums(g + 1)
                                if u == 2:
                                    weigh_sums(g + 1)
                            gather_sums(g, UNITS - 1)
                        turn_sums(GROUPS + 1)
                        weigh_sums(GROUPS + 1)
            close_pass()

        with ExitStack() as stage:
            gained = stage.enter_context(nc.sbuf_tensor("gained", [PN, NT, D], f32))
            with nc.Block() as block:
                per = 16
                batches = [(b, min(per, NT - b)) for b in range(0, NT, per)]

                @block.tensor
                def _(pe):
                    for i, (b, n) in enumerate(batches):
                        if i >= 2:
                            pe.wait_ge(last_taken, i - 1)
                        for t in range(n):
                            last = pe.transpose(banks[i % 2][0:PN, t * D:(t + 1) * D],
                                                acc[0:D, b + t:b + t + (PN - 1) * NT + 1:NT], ident[0:D, 0:D])
                        last.then_inc(last_turned, 1)

                @block.vector
                def _(dve):
                    link = Chain(dve, last_chain)
                    for i, (b, n) in enumerate(batches):
                        dve.wait_ge(last_turned, i + 1)
                        dve.tensor_scalar(gained[:, b:b + n, :], banks[i % 2][0:PN, 0:n * D].rearrange("p (t d) -> p t d", d=D),
                                          0.0, None, ALU.max).then_inc(last_taken, 1)
                    dve.wait_ge(last_taken, len(batches))
                    link(dve.tensor_tensor(xb[:, :, :], xb[:, :, :], gained[:, :, :], ALU.add))

                @block.sync
                def _(sp):
                    sp.wait_ge(last_chain, 1)
                    sp.dma_start(out.rearrange("(p t) d -> p (t d)", t=NT), xb[:, :, :].rearrange("p t d -> p (t d)"))\
                      .then_inc(stored_out, 16)
                    sp.wait_ge(stored_out, 16)


_INS = ["x", "src", "dst", "edge_type_86", "node_vec1", "node_vec1_n2", "L1_gnn_weight", "L1_gnn_w_comp",
        "L1_gnn_self_loop_weight", "L1_gnn_A1_w", "L1_gnn_A1_b", "L1_gnn_A2_w", "L1_gnn_A2_b", "L1_gnn_rel_emb"]


def kernel(**inputs):
    import numpy as _np
    import concourse.bacc as _bacc
    from concourse import mybir as _mybir
    from concourse.bass_utils import run_bass_kernel_spmd as _run

    nc = _bacc.Bacc("TRN2", target_bir_lowering=False, num_devices=1)
    arrays, args = {}, []
    for name in _INS:
        a = _np.ascontiguousarray(inputs[name])
        arrays[f"in_{name}"] = a
        args.append(nc.dram_tensor(f"in_{name}", a.shape, _mybir.dt.from_np(a.dtype), kind="ExternalInput").ap())
    out = nc.dram_tensor("out_0", inputs["x"].shape, _mybir.dt.float32, kind="ExternalOutput").ap()
    gnn_kernel(nc, *args, out)
    r = _run(nc, [arrays], core_ids=[0])
    return r.results[0]["out_0"]
```

```python
import concourse.bass as bass
from concourse import mybir
from contextlib import ExitStack



def gnn_kernel(nc, x, src, dst, etype, cj, ci, weight, w_comp, w_self, a1_w, a1_b, a2_w, a2_b, rel_emb, out):
    f32 = mybir.dt.float32
    bf16 = mybir.dt.bfloat16
    f16 = mybir.dt.float16
    i32 = mybir.dt.int32
    ALU = mybir.AluOpType
    ACT = mybir.ActivationFunctionType
    AX = mybir.AxisListType.X

    N, D = x.shape
    E = src.shape[0]
    R, NB = w_comp.shape
    GROUPS = 125
    GE = E // GROUPS
    CH = GE // 128
    UNITS = 5
    UC = CH // UNITS
    UE = UC * 128
    WIN = 128
    SLOTS = 8
    QR = 4
    QC = -(-CH // QR)
    QS = QC * SLOTS
    TILES = -(-N // WIN)
    PN = 125
    NT = N // PN
    NPAD = N + WIN
    BIG = 1.0e6
    EPS = 1e-5
    YC = D + NB
    CC = NB + 1
    ZC = SLOTS * CC
    ZB = 512 // ZC
    F0 = 3 * D
    GUNITS, GUC = 4, 3
    CG = GUNITS * GUC
    CD = CH - CG
    HOTC = NT * SLOTS
    assert E == GROUPS * GE and GE == 128 * CH and CH == UNITS * UC and N == PN * NT and QR * D == 128
    assert GROUPS % 2 == 1 and HOTC <= 1024 and NT % 2 == 0

    table0 = nc.dram_tensor("table0", [N, F0], bf16).ap()
    table1 = nc.dram_tensor("table1", [N, 2 * D], f32).ap()
    dst_table = nc.dram_tensor("dst_table", [NPAD, 3 * D], bf16).ap()
    keys = nc.dram_tensor("keys", [2 * GROUPS, GE], f32).ap()
    key_rows = nc.dram_tensor("key_rows", [GROUPS, GE], bf16).ap()
    last_marks = nc.dram_tensor("last_marks", [E + TILES * WIN, 1], f32).ap()
    type_rows = nc.dram_tensor("type_rows", [GROUPS, GE], bf16).ap()

    ctx = ExitStack()
    with ctx:
        def sb(name, shape, dt):
            return ctx.enter_context(nc.sbuf_tensor(name, shape, dt))

        acc = sb("acc", [128, NPAD], f32)
        xb = sb("xb", [PN, NT, D], f32)
        srcT = sb("srcT", [128, GROUPS + 1, CH], i32)
        slotT = sb("slotT", [128, GROUPS, CH], f32)
        nodeT = sb("nodeT", [QS, QR, GROUPS + 1], f32)
        ident = sb("ident", [128, 128], f32)
        iota_r = sb("iota_r", [128, 128], f32)
        iota_p = sb("iota_p", [128, 1], f32)
        base_col = sb("base_col", [128, 1], f32)
        left_col = sb("left_col", [128, 1], f32)
        base_f = sb("base_f", [1, GROUPS + 1], f32)
        base_i = sb("base_i", [1, GROUPS + 1], i32)
        passes_f = sb("passes_f", [1, 1], f32)
        passes_i = sb("passes_i", [1, 1], i32)
        more = sb("more", [1, 1], f32)
        order_col = sb("order_col", [128, 1], f32)
        mixed = sb("mixed", [1, 1], f32)
        mixed_i = sb("mixed_i", [1, 1], i32)
        cjt = sb("cjt", [PN, NT], f32)
        cit = sb("cit", [PN, NT], f32)
        mean = sb("mean", [PN, NT], f32)
        var = sb("var", [PN, NT], f32)
        std = sb("std", [PN, NT], f32)
        sum_w = sb("sum_w", [F0, D], f32)
        both_a = sb("both_a", [128, 4, 2 * D], f32)
        b1_row = sb("b1_row", [128, D], f32)
        b2_row = sb("b2_row", [128, D], f32)
        w_diag = sb("w_diag", [128, CC, QR, D], f32)
        type_tab = sb("type_tab", [R, YC], f32)
        type_left = sb("type_left", [R, YC], f32)
        type_tabs = sb("type_tabs", [R, 3, YC], bf16)
        pairs = [ctx.enter_context(nc.psum_tensor(f"pair{i}", [128, 2, 512], f32)) for i in range(4)]
        banks = [pairs[i // 2][:, i % 2, :] for i in range(8)]

        def sem(name):
            return nc.alloc_semaphore(name)

        loaded = {n: sem(f"loaded_{n}") for n in
                  ("dst", "next", "last", "src", "type", "x", "cj", "ci", "small", "sums", "blocks")}
        stored = sem("stored")
        stored_pad = sem("stored_pad")
        stored_out = sem("stored_out")
        marks_done = sem("marks_done")
        marks_in = sem("marks_in")
        marks_turned = sem("marks_turned")
        marks_copied = sem("marks_copied")
        zero_marks = sem("zero_marks")
        ln_in = sem("ln_in")
        iota_done = sem("iota_done")
        consts_done = sem("consts_done")
        prep_chain = sem("prep_chain")
        keys_done = sem("keys_done")
        types_done = sem("types_done")
        src_f_done = sem("src_f_done")
        cols_done = sem("cols_done")
        cols_turned = sem("cols_turned")
        src_turned = sem("src_turned")
        src_copied = sem("src_copied")
        ln_chain = sem("ln_chain")
        ln_var = sem("ln_var")
        ln_std = sem("ln_std")
        table0_done = sem("table0_done")
        agg_made = sem("agg_made")
        agg_taken = sem("agg_taken")
        mid_chain = sem("mid_chain")
        h_done = sem("h_done")
        h_turned = sem("h_turned")
        h_copied = sem("h_copied")
        a_made = sem("a_made")
        a_taken = sem("a_taken")
        tables_done = sem("tables_done")
        last_turned = sem("last_turned")
        last_taken = sem("last_taken")
        last_chain = sem("last_chain")
        restart = sem("restart")
        split_chain = sem("split_chain")
        cols_iota = sem("cols_iota")

        scan_in = sem("scan_in")
        scan_free = sem("scan_free")
        scan_chain = sem("scan_chain")
        scan_ready = sem("scan_ready")
        scan_set = sem("scan_set")
        scan_mark = sem("scan_mark")
        of_scan = range(scan_in.num, scan_mark.num + 1)

        keys_in = sem("keys_in")
        prep_link = sem("prep_link")
        key_rounded = sem("key_rounded")
        key_rows_out = sem("key_rows_out")
        left_done = sem("left_done")
        left_out = sem("left_out")
        slots_made = sem("slots_made")
        nodes_made = sem("nodes_made")
        cols_made = sem("cols_made")
        prep_turned = sem("prep_turned")
        nodes_turned = sem("nodes_turned")
        nodes_copied = sem("nodes_copied")
        slots_turned = sem("slots_turned")
        slots_copied = sem("slots_copied")
        idx_ready = sem("idx_ready")
        slot_free = sem("slot_free")
        pool_turn = sem("pool_turn")
        pe_turn = sem("pe_turn")
        rows_free = sem("rows_free")
        hot_ready = sem("hot_ready")
        table_in = sem("table_in")
        bank_zero = sem("bank_zero")
        columns_ready = sem("columns_ready")
        counts_made = sem("counts_made")
        counts_copied = sem("counts_copied")
        counted_summed = sem("counted_summed")
        dve_chain = sem("dve_chain")
        nodes_hot = sem("nodes_hot")
        sums_ready = sem("sums_ready")
        sums_free = sem("sums_free")
        y_ready = sem("y_ready")
        y_free = sem("y_free")
        score_ready = sem("score_ready")
        att_ready = sem("att_ready")
        factors_ready = sem("factors_ready")
        win_in = sem("win_in")
        win_free = sem("win_free")
        part_copied = sem("part_copied")
        slot_sums_made = sem("slot_sums_made")
        slot_sums_copied = sem("slot_sums_copied")
        key_in = [sem(f"key_in{u}") for u in range(UNITS)]
        type_in = [sem(f"type_in{u}") for u in range(UNITS)]
        gathered = [sem(f"gathered{u}") for u in range(UNITS)]
        of_pass = range(keys_in.num, gathered[-1].num + 1)
        of_gathers = range(gathered[0].num, gathered[-1].num + 1)

        class Chain:

            def __init__(self, engine, s, start=0):
                self.engine, self.s, self.start, self.n = engine, s, start, 0

            def __call__(self, ins):
                ins.then_inc(self.s, 1)
                self.n += 1
                self.engine.wait_ge(self.s, self.start + self.n)

        def along(col, n):
            return col.unsqueeze(2).to_broadcast([col.shape[0], col.shape[1], n])

        passes_end = nc.alloc_registers("passes_end")

        with ExitStack() as stage:
            def tmp(name, shape, dt):
                return stage.enter_context(nc.sbuf_tensor(name, shape, dt))

            next_i = tmp("next_i", [GROUPS, GE], i32)
            dst_i, src_i, type_i = (acc[0:GROUPS, i * GE:(i + 1) * GE].bitcast(i32) for i in range(3))
            dst_f = tmp("dst_f", [GROUPS, GE], f32)
            src_f = tmp("src_f", [GROUPS, GE], f32)
            marks = tmp("marks", [GROUPS, GE], f32)
            type_b = tmp("type_b", [GROUPS, GE], bf16)
            full = (GROUPS - 1) * GE
            with nc.allow_non_contiguous_dma(reason="transposed 32 x 32 weights, once"), nc.Block() as block:
                @block.sync
                def _(sp):
                    sp.dma_start(dst_i[:, :], dst.rearrange("(g e) -> g e", e=GE)).then_inc(loaded["dst"], 16)
                    sp.wait_ge(consts_done, 1)
                    sp.dma_start(next_i[0:GROUPS - 1, :], dst[1:full + 1].rearrange("(g e) -> g e", e=GE)).then_inc(loaded["next"], 16)
                    sp.dma_start(next_i[GROUPS - 1:GROUPS, 0:GE - 1], dst[full + 1:E].rearrange("(g e) -> g e", e=GE - 1))\
                      .then_inc(loaded["last"], 16)
                    sp.dma_start(src_i[:, :], src.rearrange("(g e) -> g e", e=GE)).then_inc(loaded["src"], 16)
                    sp.dma_start(type_i, etype.rearrange("(g e) -> g e", e=GE)).then_inc(loaded["type"], 16)
                    sp.dma_start(xb[:, :, :], x.rearrange("(p t) d -> p t d", t=NT)).then_inc(loaded["x"], 16)
                    sp.dma_start(cjt[:, :], cj.rearrange("(p t) o -> p (t o)", t=NT)).then_inc(loaded["cj"], 16)
                    sp.dma_start(cit[:, :], ci.rearrange("(p t) o -> p (t o)", t=NT)).then_inc(loaded["ci"], 16)
                    sp.wait_ge(keys_done, 1)
                    sp.dma_start(keys[0:GROUPS, :], dst_f[:, :]).then_inc(stored, 16)
                    sp.wait_ge(marks_done, 1)
                    sp.dma_start(last_marks[0:E, :].rearrange("(g e) o -> g (e o)", e=GE), marks[:, :]).then_inc(stored, 16)
                    sp.wait_ge(types_done, 1)
                    sp.dma_start(type_rows, type_b[:, :]).then_inc(stored, 16)
                    for n in ("x", "cj", "ci"):
                        sp.wait_ge(loaded[n], 16)
                    sp.wait_ge(stored, 48)

                @block.scalar
                def _(act):
                    act.wait_ge(consts_done, 2)
                    small = [
                        (both_a[0:D, 0, 0:D], a1_w.rearrange("a i -> i a")),
                        (both_a[0:D, 0, D:2 * D], a2_w.rearrange("a i -> i a")),
                        (b1_row[:, :], a1_b.rearrange("(o a) -> o a", o=1).to_broadcast([128, D])),
                        (b2_row[:, :], a2_b.rearrange("(o a) -> o a", o=1).to_broadcast([128, D])),
                        (type_tab[:, 0:D], rel_emb),
                        (type_tab[:, D:D + NB], w_comp),
                    ]
                    for q in range(QR):
                        small.append((w_diag[q * D:(q + 1) * D, 0:NB, q, :], weight.rearrange("b i o -> i b o")))
                        small.append((w_diag[q * D:(q + 1) * D, NB, q, :], w_self))
                    for to, of in small:
                        act.dma_start(to, of).then_inc(loaded["small"], 16)
                    act.wait_ge(consts_done, 3)
                    for part in range(3):
                        act.dma_start(sum_w[part * D:(part + 1) * D, :], ident[0:D, 0:D]).then_inc(loaded["sums"], 16)
                    act.wait_ge(loaded["sums"], 48)
                    act.wait_ge(loaded["small"], 16 * (6 + 2 * QR))
                    for q in range(1, 4):
                        act.dma_start(both_a[q * D:(q + 1) * D, q, :], both_a[0:D, 0, :]).then_inc(loaded["blocks"], 16)
                    act.wait_ge(loaded["blocks"], 48)

                @block.gpsimd
                def _(pool):
                    opt = dict(allow_small_or_imprecise_dtypes=True)
                    pool.iota(iota_r[:, :], [[1, 128]], base=0, channel_multiplier=0, **opt).then_inc(iota_done, 1)
                    pool.iota(iota_p[:, :], [[0, 1]], base=0, channel_multiplier=1, **opt).then_inc(iota_done, 1)
                    pool.wait_ge(iota_done, 2)

                @block.vector
                def _(dve):
                    link = Chain(dve, prep_chain)
                    dve.memset(next_i[:, :], int(BIG)).then_inc(consts_done, 1)
                    for t in (base_f, w_diag, both_a):
                        link(dve.memset(t[tuple([slice(None)] * len(t.shape))], 0.0))
                    link(dve.memset(nodeT[:, :, 0], -1.0))
                    link(dve.memset(passes_f[:, :], 1.0))
                    dve.memset(srcT[:, GROUPS, :], 0).then_inc(consts_done, 1)
                    dve.wait_ge(iota_done, 2)
                    dve.tensor_scalar(ident[:, :], iota_r[:, :], iota_p[:, 0:1], None, ALU.is_equal)\
                       .then_inc(consts_done, 1)
                    dve.wait_ge(loaded["dst"], 16)
                    dve.tensor_copy(dst_f[:, :], dst_i[:, :]).then_inc(keys_done, 1)
                    dve.wait_ge(loaded["src"], 16)
                    dve.tensor_copy(src_f[:, :], src_i[:, :]).then_inc(src_f_done, 1)
                    dve.wait_ge(loaded["next"], 16)
                    dve.wait_ge(loaded["last"], 16)
                    link(dve.tensor_tensor(marks[:, :], next_i[:, :], dst_i[:, :], ALU.subtract))
                    dve.tensor_reduce(order_col[0:GROUPS, :], marks[:, :], AX, ALU.min).then_inc(cols_done, 1)
                    dve.wait_ge(cols_done, 1)
                    dve.tensor_scalar(marks[:, :], marks[:, :], 0.0, None, ALU.not_equal).then_inc(marks_done, 1)
                    dve.wait_ge(loaded["type"], 16)
                    dve.tensor_copy(type_b[:, :], type_i).then_inc(types_done, 1)
                    dve.wait_ge(loaded["small"], 16 * (6 + 2 * QR))
                    link(dve.tensor_tensor(type_tab[:, 0:D], type_tab[:, 0:D], b2_row[0:R, :], ALU.add))
                    link(dve.tensor_copy(type_tabs[:, 0, :], type_tab[:, :]))
                    link(dve.tensor_tensor(type_left[:, :], type_tab[:, :], type_tabs[:, 0, :], ALU.subtract))
                    link(dve.tensor_copy(type_tabs[:, 1, :], type_left[:, :]))
                    link(dve.tensor_tensor(type_left[:, :], type_left[:, :], type_tabs[:, 1, :], ALU.subtract))
                    link(dve.tensor_copy(type_tabs[:, 2, :], type_left[:, :]))
                    dve.wait_ge(cols_turned, 1)
                    link(dve.tensor_reduce(mixed[:, :], banks[2][0:1, 0:GROUPS], AX, ALU.min))
                    link(dve.tensor_scalar(mixed[:, :], mixed[:, :], 0.0, None, ALU.is_lt))
                    link(dve.tensor_copy(mixed_i[:, :], mixed[:, :]))
                    for b in range(0, CH, 4):
                        n = min(4, CH - b)
                        dve.wait_ge(src_turned, b // 4 + 1)
                        dve.tensor_copy(srcT[:, 0:GROUPS, b:b + n].rearrange("p g k -> p k g"),
                                        banks[b // 4 % 2][:, 0:n * GROUPS].rearrange("p (k g) -> p k g", g=GROUPS))\
                           .then_inc(src_copied, 1)

                @block.tensor
                def _(pe):
                    pe.wait_ge(consts_done, 3)
                    pe.wait_ge(cols_done, 1)
                    pe.transpose(banks[2][0:1, 0:GROUPS], order_col[0:GROUPS, :], ident[0:GROUPS, 0:GROUPS]).then_inc(cols_turned, 1)
                    pe.wait_ge(src_f_done, 1)
                    for b in range(0, CH, 4):
                        n = min(4, CH - b)
                        if b >= 8:
                            pe.wait_ge(src_copied, b // 4 - 1)
                        for k in range(n):
                            last = pe.transpose(banks[b // 4 % 2][:, k * GROUPS:(k + 1) * GROUPS],
                                                src_f[:, (b + k) * 128:(b + k + 1) * 128], ident[0:GROUPS, 0:GROUPS])
                        last.then_inc(src_turned, 1)

        dst_mixed = nc.values_load(mixed_i[0:1, 0:1], min_val=0, max_val=1)
        with nc.If(dst_mixed > 0):
            with ExitStack() as stage:
                def tmp(name, shape, dt):
                    return stage.enter_context(nc.sbuf_tensor(name, shape, dt))

                local_e = tmp("local_e", [128, GE], f32)
                row = tmp("scan_row", [128, GE], f32)
                found = tmp("found", [128, GE], f32)
                zero = tmp("zero", [128, (E + TILES * WIN) // 128], f32)
                node = tmp("node", [128, 1], f32)
                group_max = tmp("group_max", [128, 1], f32)
                in_all = tmp("in_all", [128, 1], f32)
                ofs = tmp("ofs", [128, 1], f32)
                last = tmp("last", [128, 1], f32)
                none = tmp("none", [128, 1], f32)
                spot = tmp("spot", [128, 1], i32)
                one = tmp("one", [128, 1], f32)
                with nc.Block() as block:
                    @block.gpsimd
                    def _(pool):
                        pool.iota(local_e[:, :], [[1, GE]], base=1, channel_multiplier=0,
                                  allow_small_or_imprecise_dtypes=True).then_inc(zero_marks, 1)
                        pool.memset(zero[:, :], 0.0).then_inc(zero_marks, 1)
                        pool.memset(one[:, :], 1.0).then_inc(zero_marks, 1)
                        pool.memset(node[:, :], 0.0).then_inc(zero_marks, 1)
                        pool.wait_ge(zero_marks, 4)

                    @block.vector
                    def _(dve):
                        dve.wait_ge(zero_marks, 4)
                        dve.tensor_copy(node[:, :], iota_p[:, :]).then_inc(zero_marks, 1)
                        dve.wait_ge(zero_marks, 5)

                    @block.scalar
                    def _(act):
                        act.wait_ge(zero_marks, 4)

                    @block.tensor
                    def _(pe):
                        pe.wait_ge(zero_marks, 4)

                    @block.sync
                    def _(sp):
                        sp.wait_ge(zero_marks, 4)
                        sp.dma_start(last_marks.rearrange("(p a) o -> p (a o)", p=128), zero[:, :]).then_inc(stored_pad, 16)
                        sp.wait_ge(stored_pad, 16)

                with nc.Fori(0, TILES) as _t:
                    with nc.Block() as block:
                        @block.sync
                        def _(sp):
                            with sp.Fori(0, GROUPS) as g:
                                sp.wait_ge(scan_free, g + 1)
                                sp.dma_start(row[:, :], keys[bass.ds(g, 1), :].to_broadcast([128, GE])).then_inc(scan_in, 16)

                        @block.vector
                        def _(dve):
                            pre = Chain(dve, scan_chain)
                            pre(dve.memset(last[:, :], 0.0))
                            pre(dve.memset(ofs[:, :], 0.0))
                            dve.sem_inc(scan_free, 1)
                            with dve.Fori(0, GROUPS) as g:
                                link = Chain(dve, scan_chain, 5 * g + 2)
                                dve.wait_ge(scan_in, 16 * g + 16)
                                link(dve.scalar_tensor_tensor(found[:, :], row[:, :], node[:, 0:1], local_e[:, :],
                                                              ALU.is_equal, ALU.mult))
                                dve.sem_inc(scan_free, 1)
                                link(dve.tensor_reduce(group_max[:, :], found[:, :], AX, ALU.max))
                                link(dve.tensor_scalar(in_all[:, :], group_max[:, :], 0.0, ofs[:, 0:1], ALU.is_gt, ALU.mult))
                                link(dve.scalar_tensor_tensor(last[:, :], in_all[:, :], group_max[:, 0:1], last[:, :], ALU.add, ALU.max))
                                link(dve.tensor_scalar(ofs[:, :], ofs[:, :], float(GE), None, ALU.add))
                            post = Chain(dve, scan_ready)
                            post(dve.tensor_scalar(none[:, :], last[:, :], 0.0, float(E + 1), ALU.is_equal, ALU.mult))
                            post(dve.tensor_scalar(in_all[:, :], last[:, :], 0.0, node[:, 0:1], ALU.is_equal, ALU.mult))
                            post(dve.tensor_tensor(none[:, :], none[:, :], in_all[:, :], ALU.add))
                            post(dve.scalar_tensor_tensor(none[:, :], last[:, :], -1.0, none[:, :], ALU.add, ALU.add))
                            post(dve.tensor_copy(spot[:, :], none[:, :]))
                            post(dve.tensor_scalar(node[:, :], node[:, :], float(WIN), None, ALU.add))

                        @block.gpsimd
                        def _(pool):
                            pool.wait_ge(scan_ready, 5)
                            pool.indirect_dma_start(last_marks, bass.IndirectOffsetOnAxis(ap=spot[:, 0:1], axis=0), one[:, :], None)\
                                .then_inc(scan_mark, 16)
                            pool.wait_ge(scan_mark, 16)
                    nc.gpsimd.dma_reset(range(scan_mark.num, scan_mark.num + 1))
                    nc.all_engine_barrier(sems_to_clear=of_scan)

        def layer_norm(dve, link, to, of, scratch, vars_before):
            link(dve.tensor_reduce(mean[:, :], of, AX, ALU.add))
            link(dve.tensor_scalar(mean[:, :], mean[:, :], 1.0 / D, None, ALU.mult))
            link(dve.tensor_tensor(to, of, along(mean[:, :], D), ALU.subtract))
            link(dve.tensor_tensor(scratch, to, to, ALU.mult))
            link(dve.tensor_reduce(var[:, :], scratch, AX, ALU.add))
            dve.tensor_scalar(var[:, :], var[:, :], 1.0 / D, EPS, ALU.mult, ALU.add).then_inc(ln_var, 1)
            dve.wait_ge(ln_std, vars_before + 1)
            link(dve.reciprocal(std[:, :], std[:, :]))
            link(dve.tensor_tensor(to, to, along(std[:, :], D), ALU.mult))
            link(dve.tensor_scalar(to, to, 0.0, None, ALU.max))

        def take_root(act, n):
            act.wait_ge(ln_var, n)
            act.activation(std[:, :], var[:, :], ACT.Sqrt).then_inc(ln_std, 1)

        of_layer0 = ctx.enter_context(ExitStack())

        def sb0(name, shape, dt):
            return of_layer0.enter_context(nc.sbuf_tensor(name, shape, dt))

        placeT = sb0("placeT", [128, GROUPS, CD], f32)
        stepT = sb0("stepT", [128, GROUPS, CD], f32)
        columnT = sb0("columnT", [128, GROUPS, CD], f32)
        iota_cols = sb0("iota_cols", [128, HOTC], f16)
        with ExitStack() as stage:
            near_i = stage.enter_context(nc.sbuf_tensor("near_i", [128, GROUPS, CD], i32))
            over = stage.enter_context(nc.sbuf_tensor("over", [128, GROUPS, CD], f32))
            cols_f = stage.enter_context(nc.sbuf_tensor("cols_f", [128, HOTC], f32))
            with nc.Block() as block:
                @block.gpsimd
                def _(pool):
                    pool.iota(cols_f[:, :], [[1, HOTC]], base=0, channel_multiplier=0,
                              allow_small_or_imprecise_dtypes=True).then_inc(cols_iota, 1)
                    pool.wait_ge(cols_iota, 1)

                @block.vector
                def _(dve):
                    link = Chain(dve, split_chain)
                    of = srcT[:, 0:GROUPS, CG:CH]
                    link(dve.tensor_scalar(placeT[:, :, :], of, 1.0 / NT, None, ALU.mult))
                    link(dve.tensor_copy(near_i[:, :, :], placeT[:, :, :]))
                    link(dve.tensor_copy(placeT[:, :, :], near_i[:, :, :]))
                    link(dve.scalar_tensor_tensor(stepT[:, :, :], placeT[:, :, :], -float(NT), of, ALU.mult, ALU.add))
                    for limit, by in ((0.0, -1.0), (float(NT), 1.0)):
                        link(dve.tensor_scalar(over[:, :, :], stepT[:, :, :], limit, by, ALU.is_lt if by < 0 else ALU.is_ge, ALU.mult))
                        link(dve.tensor_tensor(placeT[:, :, :], placeT[:, :, :], over[:, :, :], ALU.add))
                        link(dve.scalar_tensor_tensor(stepT[:, :, :], over[:, :, :], -float(NT), stepT[:, :, :], ALU.mult, ALU.add))
                    link(dve.tensor_scalar(stepT[:, :, :], stepT[:, :, :], float(SLOTS), None, ALU.mult))
                    dve.wait_ge(cols_iota, 1)
                    link(dve.tensor_copy(iota_cols[:, :], cols_f[:, :]))

        with ExitStack() as stage:
            h = stage.enter_context(nc.sbuf_tensor("h0", [PN, NT, D], f32))
            scratch = stage.enter_context(nc.sbuf_tensor("scratch0", [PN, NT, D], f32))
            parts = stage.enter_context(nc.sbuf_tensor("parts0", [PN, NT, 3, D], bf16))
            with nc.Block() as block:
                @block.gpsimd
                def _(pool):
                    pool.memset(acc[0:D, :], 0.0).then_inc(iota_done, 1)
                    pool.wait_ge(iota_done, 3)

                @block.scalar
                def _(act):
                    take_root(act, 1)

                @block.vector
                def _(dve):
                    link = Chain(dve, ln_chain)
                    layer_norm(dve, link, h[:, :, :], xb[:, :, :], scratch[:, :, :], 0)
                    link(dve.tensor_tensor(h[:, :, :], h[:, :, :], along(cjt[:, :], D), ALU.mult))
                    link(dve.tensor_copy(parts[:, :, 0, :], h[:, :, :]))
                    link(dve.tensor_tensor(h[:, :, :], h[:, :, :], parts[:, :, 0, :], ALU.subtract))
                    link(dve.tensor_copy(parts[:, :, 1, :], h[:, :, :]))
                    link(dve.tensor_tensor(h[:, :, :], h[:, :, :], parts[:, :, 1, :], ALU.subtract))
                    dve.tensor_copy(parts[:, :, 2, :], h[:, :, :]).then_inc(table0_done, 1)

                @block.sync
                def _(sp):
                    sp.wait_ge(table0_done, 1)
                    sp.dma_start(table0.rearrange("(p t) f -> p (t f)", t=NT),
                                 parts[:, :, :, :].rearrange("p t s d -> p (t s d)")).then_inc(stored, 16)
                    sp.wait_ge(stored, 64)

        def prepare_pass(p, layer):
            with ExitStack() as stage:
                def tmp(name, shape, dt):
                    return stage.enter_context(nc.sbuf_tensor(name + str(layer), shape, dt))

                left = tmp("left", [GROUPS, GE], f32)
                key = tmp("key", [GROUPS, GE], f32)
                key_b = tmp("key_b", [GROUPS, GE], bf16)
                slot = tmp("slot", [GROUPS, GE], f32)
                taken = tmp("taken", [GROUPS, GE], f32)
                least = tmp("least", [GROUPS, QC * QR], f32)
                nodes = tmp("nodes", [GROUPS, QR, QC, SLOTS], f32)
                with nc.Block() as block:
                    @block.sync
                    def _(sp):
                        version = (p + 127) // 128 * GROUPS
                        sp.dma_start(left[:, :], keys[bass.ds(version, GROUPS), :]).then_inc(keys_in, 16)
                        sp.wait_ge(key_rounded, 1)
                        sp.dma_start(key_rows, key_b[:, :]).then_inc(key_rows_out, 16)
                        sp.wait_ge(left_done, 1)
                        sp.dma_start(keys[GROUPS:2 * GROUPS, :], left[:, :]).then_inc(left_out, 16)
                        sp.wait_ge(key_rows_out, 16)
                        sp.wait_ge(left_out, 16)

                    @block.vector
                    def _(dve):
                        link = Chain(dve, prep_link)
                        chunks = key[:, :].rearrange("g (k e) -> g k e", e=128)
                        by_set = (least[:, :].rearrange("g (q c) -> g q c", q=QR) if layer == 0
                                  else least[:, :].rearrange("g (c q) -> g q c", q=QR))
                        link(dve.memset(least[:, CH:QC * QR], -1000.0))
                        dve.wait_ge(keys_in, 16)
                        link(dve.tensor_reduce(base_col[0:GROUPS, :], left[:, :], AX, ALU.min))
                        link(dve.tensor_scalar(base_col[0:GROUPS, :], base_col[0:GROUPS, :], float(N - 1), None, ALU.min))
                        link(dve.tensor_scalar(key[:, :], left[:, :], base_col[0:GROUPS, 0:1], None, ALU.subtract))
                        link(dve.tensor_reduce(least[:, 0:CH], chunks, AX, ALU.min))
                        link(dve.tensor_scalar(least[:, 0:CH], least[:, 0:CH], 255.0, None, ALU.min))
                        dve.tensor_tensor(slot[:, :].rearrange("g (k e) -> g k e", e=128), chunks, along(least[:, 0:CH], 128),
                                          ALU.subtract).then_inc(slots_made, 1)
                        dve.tensor_tensor(nodes[:, :, :, :],
                                          by_set.unsqueeze(3).to_broadcast([GROUPS, QR, QC, SLOTS]),
                                          iota_r[0:GROUPS, 0:SLOTS].unsqueeze(1).unsqueeze(1).to_broadcast([GROUPS, QR, QC, SLOTS]),
                                          ALU.add).then_inc(nodes_made, 1)
                        dve.tensor_copy(key_b[:, :], key[:, :]).then_inc(key_rounded, 1)
                        dve.wait_ge(slots_made, 1)
                        link(dve.tensor_scalar(taken[:, :], slot[:, :], float(SLOTS), None, ALU.is_lt))
                        link(dve.scalar_tensor_tensor(taken[:, :], key[:, :], float(WIN), taken[:, :], ALU.is_lt, ALU.mult))
                        dve.scalar_tensor_tensor(left[:, :], taken[:, :], BIG, left[:, :], ALU.mult, ALU.add).then_inc(left_done, 1)
                        dve.wait_ge(left_done, 1)
                        dve.tensor_reduce(left_col[0:GROUPS, :], left[:, :], AX, ALU.min).then_inc(cols_made, 1)
                        dve.wait_ge(prep_turned, 1)
                        link(dve.tensor_copy(base_f[:, 1:GROUPS + 1], banks[2][0:1, 0:GROUPS]))
                        link(dve.tensor_copy(base_i[:, :], base_f[:, :]))
                        link(dve.tensor_reduce(more[:, :], banks[2][0:1, 128:128 + GROUPS], AX, ALU.min))
                        link(dve.tensor_scalar(more[:, :], more[:, :], BIG / 2, None, ALU.is_lt))
                        link(dve.tensor_tensor(passes_f[:, :], passes_f[:, :], more[:, :], ALU.add))
                        link(dve.tensor_copy(passes_i[:, :], passes_f[:, :]))
                        if layer == 0:
                            mine = slotT[:, :, CG:CH]
                            dve.wait_ge(slots_copied, -(-CH // 4))
                            link(dve.tensor_scalar(columnT[:, :, :], mine, float(SLOTS), BIG, ALU.is_ge, ALU.mult))
                            link(dve.tensor_tensor(columnT[:, :, :], columnT[:, :, :], mine, ALU.add))
                            link(dve.tensor_tensor(columnT[:, :, :], columnT[:, :, :], stepT[:, :, :], ALU.add))

                    @block.tensor
                    def _(pe):
                        pe.wait_ge(slots_made, 1)
                        for b in range(0, CH, 4):
                            n = min(4, CH - b)
                            if b >= 8:
                                pe.wait_ge(slots_copied, b // 4 - 1)
                            for k in range(n):
                                last = pe.transpose(banks[b // 4 % 2][:, k * GROUPS:(k + 1) * GROUPS],
                                                    slot[:, (b + k) * 128:(b + k + 1) * 128], ident[0:GROUPS, 0:GROUPS])
                            last.then_inc(slots_turned, 1)
                        pe.wait_ge(nodes_made, 1)
                        for q in range(QR):
                            last = pe.transpose(banks[3][0:QS, q * GROUPS:(q + 1) * GROUPS],
                                                nodes[:, q, :, :].rearrange("g c s -> g (c s)"), ident[0:GROUPS, 0:GROUPS])
                        last.then_inc(nodes_turned, 1)
                        pe.wait_ge(cols_made, 1)
                        pe.transpose(banks[2][0:1, 0:GROUPS], base_col[0:GROUPS, :], ident[0:GROUPS, 0:GROUPS])
                        pe.transpose(banks[2][0:1, 128:128 + GROUPS], left_col[0:GROUPS, :], ident[0:GROUPS, 0:GROUPS])\
                          .then_inc(prep_turned, 1)

                    @block.scalar
                    def _(act):
                        for b in range(0, CH, 4):
                            n = min(4, CH - b)
                            act.wait_ge(slots_turned, b // 4 + 1)
                            act.copy(slotT[:, :, b:b + n].rearrange("p g k -> p k g"),
                                     banks[b // 4 % 2][:, 0:n * GROUPS].rearrange("p (k g) -> p k g", g=GROUPS))\
                               .then_inc(slots_copied, 1)
                        act.wait_ge(nodes_turned, 1)
                        act.copy(nodeT[:, :, 1:GROUPS + 1], banks[3][0:QS, 0:QR * GROUPS].rearrange("s (q g) -> s q g", g=GROUPS))\
                           .then_inc(nodes_copied, 1)
                        act.wait_ge(nodes_copied, 1)
            nc.regs_load(passes_end, passes_i[0:1, 0:1])

        def close_pass():
            nc.gpsimd.dma_reset(of_gathers)
            nc.all_engine_barrier(sems_to_clear=of_pass)

        def gather(pool, rows, idx, table, units, chunks):
            with pool.Fori(0, GROUPS) as g:
                for u in range(units):
                    pool.wait_ge(idx_ready, units * g + u + 1)
                    pool.wait_ge(slot_free, units * g + u + 1)
                    pool.sem_inc(pool_turn, 1)
                    for k in range(chunks):
                        pool.indirect_dma_start(rows[:, u, k, :], None, table,
                                                bass.IndirectOffsetOnAxis(ap=idx[:, u, k:k + 1], axis=0))\
                            .then_inc(gathered[u], 16)

        def window(eng, entry):
            return eng.value_load(base_i[0:1, bass.ds(entry, 1)], min_val=0, max_val=N - 1)

        def next_indices(dve, idx, g, u, n):
            dve.tensor_copy(idx[:, u, :], srcT[:, bass.ds(g, 1), u * n:(u + 1) * n].squeeze(1)).then_inc(idx_ready, 1)

        def slots_of(g, u, n):
            return (along(slotT[:, bass.ds(g, 1), u * n:(u + 1) * n].squeeze(1), SLOTS),
                    iota_r[:, 0:SLOTS].unsqueeze(1).to_broadcast([128, n, SLOTS]))

        def place_nodes(dve, node_hot, entry):
            dve.tensor_tensor(node_hot[:, :, :], along(nodeT[:, :, bass.ds(entry, 1)].rearrange("s q g -> s (q g)"), WIN),
                              iota_r[0:QS, :].unsqueeze(1).to_broadcast([QS, QR, WIN]), ALU.is_equal).then_inc(nodes_hot, 1)

        def place_sums(pe, slot_sums, node_hot, n):
            pe.wait_ge(nodes_hot, n)
            pe.wait_ge(slot_sums_copied, n)
            pe.wait_ge(sums_free, n)
            pe.sem_inc(pe_turn, 1)
            for q in range(QR):
                last = pe.matmul(banks[7][0:D, 0:WIN], slot_sums[:, q, :], node_hot[:, q, :], start=(q == 0), stop=(q == QR - 1))
            last.then_inc(sums_ready, 1)

        def add_window(dve, entry, n):
            at = window(dve, entry)
            dve.wait_ge(sums_ready, n)
            dve.wait_ge(sums_free, n)
            dve.tensor_tensor(acc[0:D, bass.ds(at, WIN)], acc[0:D, bass.ds(at, WIN)], banks[7][0:D, 0:WIN], ALU.add)\
               .then_inc(sums_free, 1)

        def two_by_two(engine, group):
            with engine.Fori(0, GROUPS // 2) as i:
                group(2 * i, 0, False)
                group(2 * i + 1, 1, False)
            group(GROUPS - 1, 0, True)

        nc.regs_mov(passes_end, 1)
        with nc.Fori(0, passes_end) as p:
            prepare_pass(p, 0)
            with ExitStack() as stage:
                def tmp(name, shape, dt):
                    return stage.enter_context(nc.sbuf_tensor(name, shape, dt))

                HOTS = max(h for h in (2, 3, 4) if 2 * CD % h == 0)
                rows = tmp("rows0", [128, GUNITS, GUC, F0], bf16)
                idx = tmp("idx0", [128, GUNITS, GUC], i32)
                hot = tmp("hot0", [128, GUNITS, GUC, SLOTS], bf16)
                table = tmp("table_sb", [PN, NT, F0], bf16)
                place_hot = tmp("place_hot", [128, HOTS, PN], bf16)
                column_hot = tmp("column_hot", [128, HOTS, HOTC], bf16)
                counts = tmp("counts", [PN, 2, NT, CD, SLOTS], bf16)
                parts_sb = tmp("parts_sb", [F0, QR * QS], f32)
                slot_sums = tmp("slot_sums0", [QS, QR, D], f32)
                node_hot = tmp("node_hot0", [QS, QR, WIN], f32)
                count_pairs, gathered_bank, slot_bank, counted_bank = pairs[0:2], banks[4], banks[5], banks[6]

                def turn_of(half, j):
                    return CD * half + j

                with nc.Block() as block:
                    @block.gpsimd
                    def _(pool):
                        gather(pool, rows, idx, table0, GUNITS, GUC)

                    @block.sync
                    def _(sp):
                        sp.dma_start(table[:, :, :].rearrange("p t f -> p (t f)"), table0.rearrange("(p t) f -> p (t f)", t=NT))\
                          .then_inc(table_in, 16)
                        sp.wait_ge(table_in, 16)

                    @block.scalar
                    def _(act):
                        def copy_counts(g, half, j):
                            act.wait_ge(counts_made, CD * g + j + 1 + HOTS)
                            act.wait_ge(counted_summed, g + 1)
                            act.copy(counts[:, half, :, j, :].rearrange("p (b t) s -> p b t s", b=2),
                                     count_pairs[turn_of(half, j) % 2][0:PN, :, 0:HOTC // 2].rearrange("p b (t s) -> p b t s", s=SLOTS))\
                               .then_inc(counts_copied, 1)

                        def copy_parts(n):
                            act.wait_ge(slot_free, GUNITS * n)
                            act.wait_ge(counted_summed, n + 1)
                            act.copy(parts_sb[:, 0:CG * SLOTS], gathered_bank[0:F0, 0:CG * SLOTS]).then_inc(part_copied, 1)
                            act.copy(parts_sb[:, CG * SLOTS:CH * SLOTS], counted_bank[0:F0, 0:CD * SLOTS]).then_inc(part_copied, 1)

                        def copy_slot_sums(n):
                            act.wait_ge(slot_sums_made, n)
                            act.copy(slot_sums[:, :, :], slot_bank[0:QS, 0:QR * D].rearrange("s (q d) -> s q d", d=D))\
                               .then_inc(slot_sums_copied, 1)

                        act.sem_inc(counts_copied, 2)
                        for j in range(CD):
                            copy_counts(0, 0, j)
                        act.wait_ge(bank_zero, 2)

                        def group(g, half, last):
                            for j in range(CD):
                                if not last:
                                    copy_counts(g + 1, 1 - half, j)
                                if j == 0:
                                    copy_parts(g + 1)
                                if j == 4:
                                    copy_slot_sums(g + 1)

                        two_by_two(act, group)
                        copy_parts(GROUPS + 1)
                        copy_slot_sums(GROUPS + 1)

                    @block.vector
                    def _(dve):
                        def hot_columns(g, half, j):
                            slot = turn_of(half, j) % HOTS
                            dve.wait_ge(counts_made, CD * g + j + 1)
                            dve.tensor_scalar(place_hot[:, slot, :], iota_cols[:, 0:PN],
                                              placeT[:, bass.ds(g, 1), j:j + 1].squeeze(1), None, ALU.is_equal).then_inc(columns_ready, 1)
                            dve.tensor_scalar(column_hot[:, slot, :], iota_cols[:, :],
                                              columnT[:, bass.ds(g, 1), j:j + 1].squeeze(1), None, ALU.is_equal).then_inc(columns_ready, 1)

                        pre = Chain(dve, dve_chain)
                        dve.memset(gathered_bank[0:F0, 0:CG * SLOTS], 0.0).then_inc(bank_zero, 1)
                        dve.memset(counted_bank[0:F0, 0:CD * SLOTS], 0.0).then_inc(bank_zero, 1)
                        pre(dve.memset(parts_sb[:, :], 0.0))
                        dve.sem_inc(sums_free, 1)
                        for u in range(GUNITS):
                            next_indices(dve, idx, 0, u, GUC)
                        for j in range(CD):
                            hot_columns(0, 0, j)

                        def group(g, half, last):
                            for j in range(CD):
                                if not last:
                                    hot_columns(g + 1, 1 - half, j)
                                if j % GUC == 0 and j // GUC < GUNITS:
                                    u = j // GUC
                                    dve.wait_ge(slot_free, GUNITS * g + u + 1)
                                    mine, each = slots_of(g, u, GUC)
                                    dve.tensor_tensor(hot[:, u, :, :], mine, each, ALU.is_equal).then_inc(hot_ready, 1)
                                if j % GUC == 2:
                                    u = j // GUC
                                    dve.wait_ge(gathered[u], 16 * GUC * g + 16 * GUC)
                                    next_indices(dve, idx, g + 1, u, GUC)
                                if j == 3:
                                    place_nodes(dve, node_hot, g)
                                if j == 10:
                                    add_window(dve, g, g + 1)

                        two_by_two(dve, group)
                        place_nodes(dve, node_hot, GROUPS)
                        add_window(dve, GROUPS, GROUPS + 1)
                        dve.wait_ge(sums_free, GROUPS + 2)

                    @block.tensor
                    def _(pe):
                        def count(g, half, j):
                            slot, pair = turn_of(half, j) % HOTS, count_pairs[turn_of(half, j) % 2]
                            pe.wait_ge(columns_ready, 2 * CD * g + 2 * j + 2)
                            pe.wait_ge(counts_copied, CD * g + j + 1)
                            for b in range(2):
                                last = pe.matmul(pair[0:PN, b, 0:HOTC // 2], place_hot[:, slot, :],
                                                 column_hot[:, slot, b * (HOTC // 2):(b + 1) * (HOTC // 2)], start=True, stop=True)
                            last.then_inc(counts_made, 1)

                        def sum_counted(g, half, ts):
                            if ts[0] == 0:
                                pe.wait_ge(counts_copied, CD * g + CD + 2)
                            for t in ts:
                                last = pe.matmul(counted_bank[0:F0, 0:CD * SLOTS], table[:, t, :],
                                                 counts[:, half, t, :, :].rearrange("p c s -> p (c s)"),
                                                 start=(t == 0), stop=(t == NT - 1))
                            if ts[-1] == NT - 1:
                                last.then_inc(counted_summed, 1)

                        def sum_gathered(g, u):
                            pe.wait_ge(hot_ready, GUNITS * g + u + 1)
                            pe.wait_ge(gathered[u], 16 * GUC * g + 16 * GUC)
                            for k in range(GUC):
                                c = u * GUC + k
                                last = pe.matmul(gathered_bank[0:F0, c * SLOTS:(c + 1) * SLOTS], rows[:, u, k, :], hot[:, u, k, :],
                                                 start=True, stop=True)
                            last.then_inc(slot_free, 1)

                        def add_parts(n):
                            pe.wait_ge(part_copied, 2 * n)
                            for q in range(QR):
                                last = pe.matmul(slot_bank[0:QS, q * D:(q + 1) * D], parts_sb[:, q * QS:(q + 1) * QS], sum_w[:, :],
                                                 start=True, stop=True)
                            last.then_inc(slot_sums_made, 1)

                        pe.sem_inc(slot_free, GUNITS)
                        pe.sem_inc(counts_made, HOTS)
                        pe.sem_inc(counted_summed, 2)
                        for j in range(CD):
                            count(0, 0, j)
                        pe.wait_ge(table_in, 16)

                        def group(g, half, last):
                            steps = CD - 1
                            for j in range(CD):
                                if not last:
                                    count(g + 1, 1 - half, j)
                                if j == 1:
                                    pe.wait_ge(part_copied, 2 * g + 2)
                                if j >= 1:
                                    sum_counted(g, half, range((j - 1) * NT // steps, j * NT // steps))
                                if j % GUC == 0 and j > 0:
                                    sum_gathered(g, j // GUC - 1)
                                if j == 2:
                                    add_parts(g + 1)
                                if j == 7:
                                    place_sums(pe, slot_sums, node_hot, g + 1)

                        two_by_two(pe, group)
                        add_parts(GROUPS + 1)
                        place_sums(pe, slot_sums, node_hot, GROUPS + 1)
            close_pass()

        of_layer0.close()

        lastT = sb("lastT", [128, GROUPS, CH], f32)
        with ExitStack() as stage:
            def tmp(name, shape, dt):
                return stage.enter_context(nc.sbuf_tensor(name, shape, dt))

            rows1 = tmp("rows1", [PN, NT, 2 * D], f32)
            row_y = tmp("row_y", [PN, NT, D], f32)
            agg = tmp("agg", [PN, NT, D], f32)
            h_turned_sb = tmp("h_turned_sb", [128, 2, PN], f32)
            with nc.sbuf_tensor("marks_again", [GROUPS, GE], f32) as marks, nc.Block() as block:
                per = 16
                batches = [(b, min(per, NT - b)) for b in range(0, NT, per)]

                @block.tensor
                def _(pe):
                    for i, (b, n) in enumerate(batches):
                        if i >= 2:
                            pe.wait_ge(agg_taken, i - 1)
                        for t in range(n):
                            last = pe.transpose(banks[i % 2][0:PN, t * D:(t + 1) * D],
                                                acc[0:D, b + t:b + t + (PN - 1) * NT + 1:NT], ident[0:D, 0:D])
                        last.then_inc(agg_made, 1)
                    pe.wait_ge(marks_in, 16)
                    for b in range(0, CH, 4):
                        n = min(4, CH - b)
                        if b >= 8:
                            pe.wait_ge(marks_copied, b // 4 - 1)
                        for k in range(n):
                            last = pe.transpose(banks[2 + b // 4 % 2][:, k * GROUPS:(k + 1) * GROUPS],
                                                marks[:, (b + k) * 128:(b + k + 1) * 128], ident[0:GROUPS, 0:GROUPS])
                        last.then_inc(marks_turned, 1)

                @block.sync
                def _(sp):
                    sp.dma_start(marks[:, :], last_marks[0:E, :].rearrange("(g e) o -> g (e o)", e=GE)).then_inc(marks_in, 16)
                    sp.wait_ge(marks_in, 16)

                @block.vector
                def _(dve):
                    link = Chain(dve, mid_chain)
                    for i, (b, n) in enumerate(batches):
                        dve.wait_ge(agg_made, i + 1)
                        made = banks[i % 2][0:PN, 0:n * D].rearrange("p (t c) -> p t c", c=D)
                        dve.tensor_tensor(agg[:, b:b + n, :], made, along(cit[:, b:b + n], D), ALU.mult).then_inc(agg_taken, 1)
                    dve.wait_ge(agg_taken, len(batches))
                    link(dve.tensor_tensor(xb[:, :, :], xb[:, :, :], agg[:, :, :], ALU.add))
                    layer_norm(dve, link, rows1[:, :, 0:D], xb[:, :, :], agg[:, :, :], 1)
                    link(dve.memset(passes_f[:, :], 1.0))

                @block.scalar
                def _(act):
                    for b in range(0, CH, 4):
                        n = min(4, CH - b)
                        act.wait_ge(marks_turned, b // 4 + 1)
                        act.copy(lastT[:, :, b:b + n].rearrange("p g k -> p k g"),
                                 banks[2 + b // 4 % 2][:, 0:n * GROUPS].rearrange("p (k g) -> p k g", g=GROUPS))\
                           .then_inc(marks_copied, 1)
                    take_root(act, 2)

            with nc.Block() as block:
                quads = NT // 4

                @block.gpsimd
                def _(pool):
                    pool.memset(acc[0:D, :], 0.0).then_inc(restart, 1)
                    pool.wait_ge(restart, 1)

                @block.tensor
                def _(pe):
                    def turn(i):
                        if i >= 2:
                            pe.wait_ge(h_copied, i - 1)
                        pe.transpose(banks[i % 2][:, 0:PN], agg[:, 4 * i:4 * i + 4, :].rearrange("p t d -> p (t d)"),
                                     ident[0:PN, 0:PN]).then_inc(h_turned, 1)

                    pe.wait_ge(h_done, 1)
                    turn(0)
                    for i in range(quads):
                        if i + 1 < quads:
                            turn(i + 1)
                        pe.wait_ge(h_copied, i + 1)
                        if i >= 2:
                            pe.wait_ge(a_taken, 2 * i - 2)
                        pe.matmul(banks[2 + i % 2][0:PN, 0:8 * D], h_turned_sb[:, i % 2, :], both_a[:, :, :].rearrange("p q a -> p (q a)"),
                                  start=True, stop=True).then_inc(a_made, 1)

                @block.scalar
                def _(act):
                    for i in range(quads):
                        act.wait_ge(h_turned, i + 1)
                        if i >= 2:
                            act.wait_ge(a_made, i - 1)
                        act.copy(h_turned_sb[:, i % 2, :], banks[i % 2][:, 0:PN]).then_inc(h_copied, 1)

                @block.vector
                def _(dve):
                    dve.tensor_copy(agg[:, :, :], rows1[:, :, 0:D]).then_inc(h_done, 1)
                    for i in range(quads):
                        dve.wait_ge(a_made, i + 1)
                        made = banks[2 + i % 2][0:PN, 0:8 * D].rearrange("p (t c) -> p t c", c=2 * D)
                        dve.tensor_tensor(rows1[:, 4 * i:4 * i + 4, D:2 * D], made[:, :, 0:D],
                                          b1_row[0:PN, :].unsqueeze(1).to_broadcast([PN, 4, D]), ALU.add).then_inc(a_taken, 1)
                        dve.tensor_copy(row_y[:, 4 * i:4 * i + 4, :], made[:, :, D:2 * D]).then_inc(a_taken, 1)
                    dve.wait_ge(a_taken, 2 * quads)

            parts = tmp("parts1", [PN, NT, 3, D], bf16)
            zeros = tmp("zeros", [WIN, 3 * D], bf16)
            with nc.Block() as block:
                @block.vector
                def _(dve):
                    link = Chain(dve, tables_done)
                    link(dve.memset(zeros[:, :], 0.0))
                    link(dve.tensor_copy(parts[:, :, 0, :], row_y[:, :, :]))
                    link(dve.tensor_tensor(row_y[:, :, :], row_y[:, :, :], parts[:, :, 0, :], ALU.subtract))
                    link(dve.tensor_copy(parts[:, :, 1, :], row_y[:, :, :]))
                    link(dve.tensor_tensor(row_y[:, :, :], row_y[:, :, :], parts[:, :, 1, :], ALU.subtract))
                    link(dve.tensor_copy(parts[:, :, 2, :], row_y[:, :, :]))

                @block.sync
                def _(sp):
                    sp.dma_start(table1.rearrange("(p t) f -> p (t f)", t=NT),
                                 rows1[:, :, :].rearrange("p t d -> p (t d)")).then_inc(stored, 16)
                    sp.wait_ge(tables_done, 6)
                    sp.dma_start(dst_table[0:N, :].rearrange("(p t) f -> p (t f)", t=NT),
                                 parts[:, :, :, :].rearrange("p t s d -> p (t s d)")).then_inc(stored, 16)
                    sp.dma_start(dst_table[N:NPAD, :], zeros[:, :]).then_inc(stored, 16)
                    sp.wait_ge(stored, 112)

        nc.regs_mov(passes_end, 1)
        with nc.Fori(0, passes_end) as p:
            prepare_pass(p, 1)
            with ExitStack() as stage:
                def tmp(name, shape, dt):
                    return stage.enter_context(nc.sbuf_tensor(name, shape, dt))

                RING = 3
                rows = tmp("rows_in1", [128, UNITS, UC, 2 * D], f32)
                idx = tmp("idx1", [128, UNITS, UC], i32)
                key_r = tmp("key_r1", [128, UNITS, UE], bf16)
                type_r = tmp("type_r1", [R, UNITS, UE], bf16)
                dst_hot = tmp("dst_hot", [128, RING, UE], bf16)
                type_hot = tmp("type_hot", [R, RING, UE], bf16)
                slot_hot = tmp("slot_hot", [128, UC, SLOTS], f32)
                prod = tmp("prod", [128, UC, D], f32)
                score = tmp("score", [128, 2, UC], f32)
                att = tmp("att", [128, 2, UC], f32)
                factors = tmp("factors", [128, UC, CC], f32)
                by_slot = tmp("by_slot", [128, RING, UC, SLOTS, CC], f32)
                win_raw = tmp("win_raw", [128, 3, D], bf16)
                win = tmp("win", [128, 3, D], bf16)
                sums_sb = tmp("sums_sb", [128, QC, ZC], f32)
                slot_sums = tmp("slot_sums1", [QS, QR, D], f32)
                node_hot = tmp("node_hot1", [QS, QR, WIN], f32)
                y_banks, sum_banks, slot_bank = banks[0:3], banks[3:6], banks[6]

                def before(u):
                    return {0: 2, 1: 2, 2: UNITS}.get(u, RING)

                assert UNITS == 5 and RING == 3 and QC == 2 * ZB + 1 and CH == QR * (QC - 1) + 1
                with nc.Block() as block:
                    @block.gpsimd
                    def _(pool):
                        gather(pool, rows, idx, table1, UNITS, UC)

                    @block.sync
                    def _(sp):
                        with sp.Fori(0, GROUPS) as g:
                            at = window(sp, g + 1)
                            sp.wait_ge(win_free, g + 1)
                            sp.dma_start(win_raw[:, :, :], dst_table[bass.ds(at, WIN), :].rearrange("p (s c) -> p s c", c=D))\
                              .then_inc(win_in, 16)
                            for u in range(UNITS):
                                sp.wait_ge(rows_free, 2 * UNITS * g + 2 * u + 2)
                                sp.dma_start(key_r[:, u, :], key_rows[bass.ds(g, 1), u * UE:(u + 1) * UE].to_broadcast([128, UE]))\
                                  .then_inc(key_in[u], 16)
                                sp.dma_start(type_r[:, u, :], type_rows[bass.ds(g, 1), u * UE:(u + 1) * UE].to_broadcast([R, UE]))\
                                  .then_inc(type_in[u], 16)

                    @block.scalar
                    def _(act):
                        def copy_slot_sums(n):
                            act.wait_ge(slot_sums_made, n)
                            act.copy(slot_sums[:, :, :], slot_bank[0:QS, 0:QR * D].rearrange("s (q d) -> s q d", d=D))\
                               .then_inc(slot_sums_copied, 1)

                        def copy_sums(b, parts, blocks):
                            act.copy(sums_sb[0:parts, b * ZB:b * ZB + blocks, :],
                                     sum_banks[b][0:parts, 0:blocks * ZC].rearrange("p (c z) -> p c z", z=ZC)).then_inc(part_copied, 1)

                        act.sem_inc(win_free, 1)
                        act.sem_inc(part_copied, 3)
                        with act.Fori(0, GROUPS) as g:
                            act.wait_ge(win_in, 16 * g + 16)
                            act.wait_ge(y_ready, UNITS * g + UNITS)
                            act.copy(win[:, :, :], win_raw[:, :, :]).then_inc(win_free, 1)
                            for u in range(UNITS):
                                act.wait_ge(score_ready, UNITS * g + u + 1)
                                act.activation(att[:, u % 2, :], score[:, u % 2, :], ACT.Tanh, scale=float(D) ** -0.5)\
                                   .then_inc(att_ready, 1)
                                if u == 2:
                                    copy_slot_sums(g + 1)
                                if u == 3:
                                    act.wait_ge(slot_free, UNITS * g + 3 + UNITS)
                                    copy_sums(0, 128, ZB)
                            act.wait_ge(slot_free, UNITS * g + 2 * UNITS)
                            copy_sums(1, 128, ZB)
                            copy_sums(2, D, 1)
                        copy_slot_sums(GROUPS + 1)

                    @block.vector
                    def _(dve):
                        pre = Chain(dve, dve_chain)
                        pre(dve.memset(sums_sb[:, :, :], 0.0))
                        dve.sem_inc(rows_free, 2 * UNITS)
                        dve.sem_inc(y_free, UNITS)
                        dve.sem_inc(sums_free, 1)
                        for u in range(UNITS):
                            next_indices(dve, idx, 0, u, UC)

                        with dve.Fori(0, GROUPS) as g:
                            link = Chain(dve, dve_chain, 2 * UNITS * g + 1)

                            def hot_rows(u):
                                dve.wait_ge(y_ready, UNITS * g + u - before(u) + 1 + UNITS)
                                dve.wait_ge(key_in[u], 16 * g + 16)
                                dve.tensor_scalar(dst_hot[:, u % RING, :], key_r[:, u, :], iota_p[:, 0:1], None, ALU.is_equal)\
                                   .then_inc(rows_free, 1)
                                dve.wait_ge(type_in[u], 16 * g + 16)
                                dve.tensor_scalar(type_hot[:, u % RING, :], type_r[:, u, :], iota_p[0:R, 0:1], None, ALU.is_equal)\
                                   .then_inc(rows_free, 1)

                            hot_rows(0)
                            for u in range(UNITS):
                                if u + 1 < UNITS:
                                    hot_rows(u + 1)
                                r, y = u % RING, y_banks[u % RING][:, 0:UC * YC].rearrange("p (k c) -> p k c", c=YC)
                                dve.wait_ge(y_ready, UNITS * g + u + 1 + UNITS)
                                dve.wait_ge(gathered[u], 16 * UC * g + 16 * UC)
                                link(dve.tensor_tensor(prod[:, :, :], rows[:, u, :, D:2 * D], y[:, :, 0:D], ALU.mult))
                                link(dve.tensor_reduce(score[:, u % 2, :], prod[:, :, :], AX, ALU.add))
                                dve.tensor_scalar(score[:, u % 2, :], score[:, u % 2, :], 0.0, None, ALU.max).then_inc(score_ready, 1)
                                mine, each = slots_of(g, u, UC)
                                dve.tensor_tensor(slot_hot[:, :, :], mine, each, ALU.is_equal)
                                dve.tensor_copy(factors[:, :, NB], lastT[:, bass.ds(g, 1), u * UC:(u + 1) * UC].squeeze(1))
                                dve.wait_ge(att_ready, UNITS * g + u + 1)
                                dve.tensor_tensor(factors[:, :, 0:NB], y[:, :, D:D + NB], along(att[:, u % 2, :], NB), ALU.mult)\
                                   .then_inc(y_free, 1)
                                dve.wait_ge(y_free, UNITS * g + u + 1 + UNITS)
                                dve.wait_ge(slot_free, UNITS * g + u - before(u) + 1 + UNITS)
                                dve.tensor_tensor(by_slot[:, r, :, :, :], slot_hot[:, :, :].unsqueeze(3).to_broadcast([128, UC, SLOTS, CC]),
                                                  factors[:, :, :].unsqueeze(2).to_broadcast([128, UC, SLOTS, CC]), ALU.mult)\
                                   .then_inc(factors_ready, 1)
                                next_indices(dve, idx, g + 1, u, UC)
                                dve.wait_ge(idx_ready, UNITS * g + u + 1 + UNITS)
                                if u == 1:
                                    place_nodes(dve, node_hot, g)
                                if u == 3:
                                    add_window(dve, g, g + 1)
                        place_nodes(dve, node_hot, GROUPS)
                        add_window(dve, GROUPS, GROUPS + 1)
                        dve.wait_ge(sums_free, GROUPS + 2)

                    @block.tensor
                    def _(pe):
                        def look_up(g, u):
                            pe.wait_ge(rows_free, 2 * UNITS * g + 2 * u + 2 + 2 * UNITS)
                            pe.wait_ge(y_free, UNITS * g + u - before(u) + 1 + UNITS)
                            for k in range(UC):
                                y, edges = y_banks[u % RING][:, k * YC:(k + 1) * YC], slice(k * 128, (k + 1) * 128)
                                for n in range(3):
                                    pe.matmul(y, type_hot[:, u % RING, edges], type_tabs[:, n, :], start=(n == 0), stop=False)
                                for n in range(3):
                                    last = pe.matmul(y[:, 0:D], dst_hot[:, u % RING, edges], win[:, n, :], start=False, stop=(n == 2))
                            last.then_inc(y_ready, 1)

                        def sum_by_slot(g, u):
                            pe.wait_ge(gathered[u], 16 * UC * g + 16 * UC)
                            pe.wait_ge(factors_ready, UNITS * g + u + 1)
                            for k in range(UC):
                                c = u * UC + k
                                q, b = c % QR, c // QR
                                if c % (QR * ZB) == 0:
                                    pe.wait_ge(part_copied, 3 * g + 1 + b // ZB)
                                last = pe.matmul(sum_banks[b // ZB][q * D:(q + 1) * D, b % ZB * ZC:(b % ZB + 1) * ZC],
                                                 rows[:, u, k, 0:D], by_slot[:, u % RING, k, :, :].rearrange("p s c -> p (s c)"),
                                                 start=True, stop=True)
                            last.then_inc(slot_free, 1)

                        def weigh(n):
                            pe.wait_ge(part_copied, 3 * n)
                            every = sums_sb[:, :, :].rearrange("p c (s f) -> p (c s) f", f=CC)
                            for f in range(CC):
                                last = pe.matmul(slot_bank[0:QS, 0:QR * D], every[:, :, f], w_diag[:, f, :, :].rearrange("p q o -> p (q o)"),
                                                 start=(f == 0), stop=(f == CC - 1))
                            last.then_inc(slot_sums_made, 1)

                        pe.sem_inc(y_ready, UNITS)
                        pe.sem_inc(slot_free, UNITS)
                        with pe.Fori(0, GROUPS) as g:
                            pe.wait_ge(win_free, g + 2)
                            for u in range(UNITS):
                                look_up(g, u)
                                if u >= 1:
                                    sum_by_slot(g, u - 1)
                                if u == 1:
                                    weigh(g + 1)
                                if u == 3:
                                    place_sums(pe, slot_sums, node_hot, g + 1)
                            sum_by_slot(g, UNITS - 1)
                        weigh(GROUPS + 1)
                        place_sums(pe, slot_sums, node_hot, GROUPS + 1)
            close_pass()

        with ExitStack() as stage:
            gained = stage.enter_context(nc.sbuf_tensor("gained", [PN, NT, D], f32))
            with nc.Block() as block:
                per = 16
                batches = [(b, min(per, NT - b)) for b in range(0, NT, per)]

                @block.tensor
                def _(pe):
                    for i, (b, n) in enumerate(batches):
                        if i >= 2:
                            pe.wait_ge(last_taken, i - 1)
                        for t in range(n):
                            last = pe.transpose(banks[i % 2][0:PN, t * D:(t + 1) * D],
                                                acc[0:D, b + t:b + t + (PN - 1) * NT + 1:NT], ident[0:D, 0:D])
                        last.then_inc(last_turned, 1)

                @block.vector
                def _(dve):
                    link = Chain(dve, last_chain)
                    for i, (b, n) in enumerate(batches):
                        dve.wait_ge(last_turned, i + 1)
                        dve.tensor_scalar(gained[:, b:b + n, :], banks[i % 2][0:PN, 0:n * D].rearrange("p (t d) -> p t d", d=D),
                                          0.0, None, ALU.max).then_inc(last_taken, 1)
                    dve.wait_ge(last_taken, len(batches))
                    link(dve.tensor_tensor(xb[:, :, :], xb[:, :, :], gained[:, :, :], ALU.add))

                @block.sync
                def _(sp):
                    sp.wait_ge(last_chain, 1)
                    sp.dma_start(out.rearrange("(p t) d -> p (t d)", t=NT), xb[:, :, :].rearrange("p t d -> p (t d)"))\
                      .then_inc(stored_out, 16)
                    sp.wait_ge(stored_out, 16)


_INS = ["x", "src", "dst", "edge_type_86", "node_vec1", "node_vec1_n2", "L1_gnn_weight", "L1_gnn_w_comp",
        "L1_gnn_self_loop_weight", "L1_gnn_A1_w", "L1_gnn_A1_b", "L1_gnn_A2_w", "L1_gnn_A2_b", "L1_gnn_rel_emb"]


def kernel(**inputs):
    import numpy as _np
    import concourse.bacc as _bacc
    from concourse import mybir as _mybir
    from concourse.bass_utils import run_bass_kernel_spmd as _run

    nc = _bacc.Bacc("TRN2", target_bir_lowering=False, num_devices=1)
    arrays, args = {}, []
    for name in _INS:
        a = _np.ascontiguousarray(inputs[name])
        arrays[f"in_{name}"] = a
        args.append(nc.dram_tensor(f"in_{name}", a.shape, _mybir.dt.from_np(a.dtype), kind="ExternalInput").ap())
    out = nc.dram_tensor("out_0", inputs["x"].shape, _mybir.dt.float32, kind="ExternalOutput").ap()
    gnn_kernel(nc, *args, out)
    r = _run(nc, [arrays], core_ids=[0])
    return r.results[0]["out_0"]
```

```python
import concourse.bass as bass
from concourse import mybir
from contextlib import ExitStack



def gnn_kernel(nc, x, src, dst, etype, cj, ci, weight, w_comp, w_self, a1_w, a1_b, a2_w, a2_b, rel_emb, out):
    f32 = mybir.dt.float32
    bf16 = mybir.dt.bfloat16
    f16 = mybir.dt.float16
    i32 = mybir.dt.int32
    ALU = mybir.AluOpType
    ACT = mybir.ActivationFunctionType
    AX = mybir.AxisListType.X

    N, D = x.shape
    E = src.shape[0]
    R, NB = w_comp.shape
    GROUPS = 125
    GE = E // GROUPS
    CH = GE // 128
    UNITS = 5
    UC = CH // UNITS
    UE = UC * 128
    WIN = 128
    SLOTS = 7
    QR = 4
    QC = -(-CH // QR)
    QS = QC * SLOTS
    TILES = -(-N // WIN)
    PN = 125
    NT = N // PN
    NPAD = N + WIN
    BIG = 1.0e6
    EPS = 1e-5
    YC = D + NB
    CC = NB + 1
    ZC = SLOTS * CC
    ZB = -(-QC // 3)
    F0 = 3 * D
    CG = 11
    GUC = 3
    GUNITS = -(-CG // GUC)
    CD = CH - CG
    HOTC = NT * SLOTS
    BY_DVE = [CD // 2]
    BY_ACT = [j for j in range(CD) if j not in BY_DVE]
    assert E == GROUPS * GE and GE == 128 * CH and CH == UNITS * UC and N == PN * NT and QR * D == 128
    assert GROUPS % 2 == 1 and CD - 1 not in BY_DVE and HOTC <= 1024 and NT % 2 == 0 and ZB * ZC <= 512

    table0 = nc.dram_tensor("table0", [N, F0], bf16).ap()
    table1 = nc.dram_tensor("table1", [N, 2 * D], f32).ap()
    dst_table = nc.dram_tensor("dst_table", [NPAD, 3 * D], bf16).ap()
    keys = nc.dram_tensor("keys", [2 * GROUPS, GE], f32).ap()
    key_rows = nc.dram_tensor("key_rows", [GROUPS, GE], bf16).ap()
    last_marks = nc.dram_tensor("last_marks", [E + TILES * WIN, 1], f32).ap()
    type_rows = nc.dram_tensor("type_rows", [GROUPS, GE], bf16).ap()

    ctx = ExitStack()
    with ctx:
        def sb(name, shape, dt):
            return ctx.enter_context(nc.sbuf_tensor(name, shape, dt))

        acc = sb("acc", [128, NPAD], f32)
        xb = sb("xb", [PN, NT, D], f32)
        srcT = sb("srcT", [128, GROUPS + 1, CH], i32)
        slotT = sb("slotT", [128, GROUPS, CH], f32)
        nodeT = sb("nodeT", [QS, 2, QR, GROUPS + 1], f32)
        ident = sb("ident", [128, 128], f32)
        iota_r = sb("iota_r", [128, 128], f32)
        iota_p = sb("iota_p", [128, 1], f32)
        base_col = sb("base_col", [128, 1], f32)
        left_col = sb("left_col", [128, 1], f32)
        base_f = sb("base_f", [1, GROUPS + 1], f32)
        base_i = sb("base_i", [1, GROUPS + 1], i32)
        passes_f = sb("passes_f", [1, 1], f32)
        passes_i = sb("passes_i", [1, 1], i32)
        more = sb("more", [1, 1], f32)
        order_col = sb("order_col", [128, 1], f32)
        mixed = sb("mixed", [1, 1], f32)
        mixed_i = sb("mixed_i", [1, 1], i32)
        cjt = sb("cjt", [PN, NT], f32)
        cit = sb("cit", [PN, NT], f32)
        mean = sb("mean", [PN, NT], f32)
        var = sb("var", [PN, NT], f32)
        std = sb("std", [PN, NT], f32)
        sum_w = sb("sum_w", [F0, D], f32)
        both_a = sb("both_a", [128, 4, 2 * D], f32)
        b1_row = sb("b1_row", [128, D], f32)
        b2_row = sb("b2_row", [128, D], f32)
        w_diag = sb("w_diag", [128, CC, QR, D], f32)
        type_tab = sb("type_tab", [R, YC], f32)
        type_left = sb("type_left", [R, YC], f32)
        type_tabs = sb("type_tabs", [R, 3, YC], bf16)
        pairs = [ctx.enter_context(nc.psum_tensor(f"pair{i}", [128, 2, 512], f32)) for i in range(4)]
        banks = [pairs[i // 2][:, i % 2, :] for i in range(8)]

        def sem(name):
            return nc.alloc_semaphore(name)

        loaded = {n: sem(f"loaded_{n}") for n in
                  ("dst", "next", "src", "type", "x", "cj", "ci", "small", "sums", "blocks")}
        stored_keys = sem("stored_keys")
        stored_marks = sem("stored_marks")
        stored_types = sem("stored_types")
        stored_table0 = sem("stored_table0")
        stored = sem("stored")
        stored_pad = sem("stored_pad")
        stored_out = sem("stored_out")
        marks_done = sem("marks_done")
        marks_in = sem("marks_in")
        marks_turned = sem("marks_turned")
        marks_copied = sem("marks_copied")
        zero_marks = sem("zero_marks")
        ln_in = sem("ln_in")
        iota_done = sem("iota_done")
        consts_done = sem("consts_done")
        prep_chain = sem("prep_chain")
        keys_done = sem("keys_done")
        types_done = sem("types_done")
        src_f_done = sem("src_f_done")
        cols_done = sem("cols_done")
        cols_turned = sem("cols_turned")
        src_turned = sem("src_turned")
        src_copied = sem("src_copied")
        ln_chain = sem("ln_chain")
        ln_var = sem("ln_var")
        ln_std = sem("ln_std")
        table0_done = sem("table0_done")
        agg_made = sem("agg_made")
        agg_taken = sem("agg_taken")
        mid_chain = sem("mid_chain")
        h_done = sem("h_done")
        h_turned = sem("h_turned")
        h_copied = sem("h_copied")
        a_made = sem("a_made")
        a_taken = sem("a_taken")
        tables_done = sem("tables_done")
        last_turned = sem("last_turned")
        last_taken = sem("last_taken")
        last_chain = sem("last_chain")
        restart = sem("restart")
        split_chain = sem("split_chain")
        guess_chain = sem("guess_chain")
        cols_chain = sem("cols_chain")

        scan_in = sem("scan_in")
        scan_free = sem("scan_free")
        scan_chain = sem("scan_chain")
        scan_ready = sem("scan_ready")
        scan_set = sem("scan_set")
        scan_mark = sem("scan_mark")
        of_scan = range(scan_in.num, scan_mark.num + 1)

        keys_in = sem("keys_in")
        prep_link = sem("prep_link")
        key_rounded = sem("key_rounded")
        key_rows_out = sem("key_rows_out")
        left_done = sem("left_done")
        left_out = sem("left_out")
        slots_made = sem("slots_made")
        nodes_made = sem("nodes_made")
        cols_made = sem("cols_made")
        prep_turned = sem("prep_turned")
        nodes_turned = sem("nodes_turned")
        nodes_copied = sem("nodes_copied")
        slots_turned = sem("slots_turned")
        slots_copied = sem("slots_copied")
        idx_ready = sem("idx_ready")
        slot_free = sem("slot_free")
        pool_turn = sem("pool_turn")
        pe_turn = sem("pe_turn")
        rows_free = sem("rows_free")
        hot_ready = sem("hot_ready")
        bank_zero = sem("bank_zero")
        columns_ready = sem("columns_ready")
        counts_made = sem("counts_made")
        counts_by_act = sem("counts_by_act")
        counts_by_dve = sem("counts_by_dve")
        counted_summed = sem("counted_summed")
        dve_chain = sem("dve_chain")
        nodes_hot = sem("nodes_hot")
        sums_ready = sem("sums_ready")
        sums_free = sem("sums_free")
        y_ready = sem("y_ready")
        y_free = sem("y_free")
        score_ready = sem("score_ready")
        att_ready = sem("att_ready")
        factors_ready = sem("factors_ready")
        win_in = sem("win_in")
        win_free = sem("win_free")
        part_copied = sem("part_copied")
        slot_sums_made = sem("slot_sums_made")
        slot_sums_copied = sem("slot_sums_copied")
        key_in = [sem(f"key_in{u}") for u in range(UNITS)]
        type_in = [sem(f"type_in{u}") for u in range(UNITS)]
        gathered = [sem(f"gathered{u}") for u in range(UNITS)]
        of_pass = range(keys_in.num, gathered[-1].num + 1)
        of_gathers = range(gathered[0].num, gathered[-1].num + 1)

        class Chain:

            def __init__(self, engine, s, start=0):
                self.engine, self.s, self.start, self.n = engine, s, start, 0

            def __call__(self, ins):
                ins.then_inc(self.s, 1)
                self.n += 1
                self.engine.wait_ge(self.s, self.start + self.n)

        def along(col, n):
            return col.unsqueeze(2).to_broadcast([col.shape[0], col.shape[1], n])

        passes_end = nc.alloc_registers("passes_end")
        prepare_again = nc.alloc_registers("prepare_again")

        with ExitStack() as stage:
            def tmp(name, shape, dt):
                return stage.enter_context(nc.sbuf_tensor(name, shape, dt))

            dst_i, src_i = (acc[0:GROUPS, i * GE:(i + 1) * GE].bitcast(i32) for i in range(2))
            marks = acc[0:GROUPS, 2 * GE:3 * GE]
            next_i = tmp("next_i", [GROUPS, 1], i32)
            dst_f = tmp("dst_f", [GROUPS, GE], f32)
            src_f = tmp("src_f", [GROUPS, GE], f32)
            with nc.allow_non_contiguous_dma(reason="transposed 32 x 32 weights, once"), nc.Block() as block:
                @block.sync
                def _(sp):
                    sp.dma_start(dst_i[:, :], dst.rearrange("(g e) -> g e", e=GE)).then_inc(loaded["dst"], 16)
                    sp.wait_ge(consts_done, 1)
                    sp.dma_start(next_i[0:GROUPS - 1, :], dst[GE:E].rearrange("(g e) -> g e", e=GE)[:, 0:1]).then_inc(loaded["next"], 16)
                    sp.dma_start(src_i[:, :], src.rearrange("(g e) -> g e", e=GE)).then_inc(loaded["src"], 16)
                    sp.dma_start(xb[:, :, :], x.rearrange("(p t) d -> p t d", t=NT)).then_inc(loaded["x"], 16)
                    sp.dma_start(cjt[:, :], cj.rearrange("(p t) o -> p (t o)", t=NT)).then_inc(loaded["cj"], 16)
                    sp.dma_start(cit[:, :], ci.rearrange("(p t) o -> p (t o)", t=NT)).then_inc(loaded["ci"], 16)
                    sp.wait_ge(keys_done, 1)
                    sp.dma_start(keys[0:GROUPS, :], dst_f[:, :]).then_inc(stored_keys, 16)
                    sp.wait_ge(marks_done, 1)
                    sp.dma_start(last_marks[0:E, :].rearrange("(g e) o -> g (e o)", e=GE), marks).then_inc(stored_marks, 16)
                    for n in ("x", "cj", "ci"):
                        sp.wait_ge(loaded[n], 16)
                    sp.wait_ge(stored_keys, 16)

                @block.scalar
                def _(act):
                    act.wait_ge(consts_done, 2)
                    small = [
                        (both_a[0:D, 0, 0:D], a1_w.rearrange("a i -> i a")),
                        (both_a[0:D, 0, D:2 * D], a2_w.rearrange("a i -> i a")),
                        (b1_row[:, :], a1_b.rearrange("(o a) -> o a", o=1).to_broadcast([128, D])),
                        (b2_row[:, :], a2_b.rearrange("(o a) -> o a", o=1).to_broadcast([128, D])),
                        (type_tab[:, 0:D], rel_emb),
                        (type_tab[:, D:D + NB], w_comp),
                    ]
                    for q in range(QR):
                        small.append((w_diag[q * D:(q + 1) * D, 0:NB, q, :], weight.rearrange("b i o -> i b o")))
                        small.append((w_diag[q * D:(q + 1) * D, NB, q, :], w_self))
                    for to, of in small:
                        act.dma_start(to, of).then_inc(loaded["small"], 16)
                    act.wait_ge(consts_done, 3)
                    for part in range(3):
                        act.dma_start(sum_w[part * D:(part + 1) * D, :], ident[0:D, 0:D]).then_inc(loaded["sums"], 16)
                    act.wait_ge(loaded["sums"], 48)
                    act.wait_ge(loaded["small"], 16 * (6 + 2 * QR))
                    for q in range(1, 4):
                        act.dma_start(both_a[q * D:(q + 1) * D, q, :], both_a[0:D, 0, :]).then_inc(loaded["blocks"], 16)
                    act.wait_ge(loaded["blocks"], 48)

                @block.gpsimd
                def _(pool):
                    opt = dict(allow_small_or_imprecise_dtypes=True)
                    pool.iota(iota_r[:, :], [[1, 128]], base=0, channel_multiplier=0, **opt).then_inc(iota_done, 1)
                    pool.iota(iota_p[:, :], [[0, 1]], base=0, channel_multiplier=1, **opt).then_inc(iota_done, 1)
                    pool.wait_ge(iota_done, 2)

                @block.vector
                def _(dve):
                    link = Chain(dve, prep_chain)
                    dve.memset(next_i[:, :], int(BIG)).then_inc(consts_done, 1)
                    for t in (base_f, w_diag, both_a):
                        link(dve.memset(t[tuple([slice(None)] * len(t.shape))], 0.0))
                    link(dve.memset(nodeT[:, :, :, 0], -1.0))
                    link(dve.memset(passes_f[:, :], 1.0))
                    dve.memset(srcT[:, GROUPS, :], 0).then_inc(consts_done, 1)
                    dve.wait_ge(iota_done, 2)
                    dve.tensor_scalar(ident[:, :], iota_r[:, :], iota_p[:, 0:1], None, ALU.is_equal)\
                       .then_inc(consts_done, 1)
                    dve.wait_ge(loaded["dst"], 16)
                    dve.tensor_copy(dst_f[:, :], dst_i[:, :]).then_inc(keys_done, 1)
                    dve.wait_ge(loaded["src"], 16)
                    dve.tensor_copy(src_f[:, :], src_i[:, :]).then_inc(src_f_done, 1)
                    dve.wait_ge(loaded["next"], 16)
                    link(dve.tensor_tensor(marks[:, 0:GE - 1], dst_i[:, 1:GE], dst_i[:, 0:GE - 1], ALU.subtract))
                    link(dve.tensor_tensor(marks[:, GE - 1:GE], next_i[:, :], dst_i[:, GE - 1:GE], ALU.subtract))
                    dve.tensor_reduce(order_col[0:GROUPS, :], marks, AX, ALU.min).then_inc(cols_done, 1)
                    dve.wait_ge(cols_done, 1)
                    dve.tensor_scalar(marks, marks, 0.0, None, ALU.not_equal).then_inc(marks_done, 1)
                    dve.wait_ge(loaded["small"], 16 * (6 + 2 * QR))
                    link(dve.tensor_tensor(type_tab[:, 0:D], type_tab[:, 0:D], b2_row[0:R, :], ALU.add))
                    link(dve.tensor_copy(type_tabs[:, 0, :], type_tab[:, :]))
                    link(dve.tensor_tensor(type_left[:, :], type_tab[:, :], type_tabs[:, 0, :], ALU.subtract))
                    link(dve.tensor_copy(type_tabs[:, 1, :], type_left[:, :]))
                    link(dve.tensor_tensor(type_left[:, :], type_left[:, :], type_tabs[:, 1, :], ALU.subtract))
                    link(dve.tensor_copy(type_tabs[:, 2, :], type_left[:, :]))
                    dve.wait_ge(cols_turned, 1)
                    link(dve.tensor_reduce(mixed[:, :], banks[2][0:1, 0:GROUPS], AX, ALU.min))
                    link(dve.tensor_scalar(mixed[:, :], mixed[:, :], 0.0, None, ALU.is_lt))
                    link(dve.tensor_copy(mixed_i[:, :], mixed[:, :]))
                    for b in range(0, CH, 4):
                        n = min(4, CH - b)
                        dve.wait_ge(src_turned, b // 4 + 1)
                        dve.tensor_copy(srcT[:, 0:GROUPS, b:b + n].rearrange("p g k -> p k g"),
                                        banks[b // 4 % 2][:, 0:n * GROUPS].rearrange("p (k g) -> p k g", g=GROUPS))\
                           .then_inc(src_copied, 1)

                @block.tensor
                def _(pe):
                    pe.wait_ge(consts_done, 3)
                    pe.wait_ge(cols_done, 1)
                    pe.transpose(banks[2][0:1, 0:GROUPS], order_col[0:GROUPS, :], ident[0:GROUPS, 0:GROUPS]).then_inc(cols_turned, 1)
                    pe.wait_ge(src_f_done, 1)
                    for b in range(0, CH, 4):
                        n = min(4, CH - b)
                        if b >= 8:
                            pe.wait_ge(src_copied, b // 4 - 1)
                        for k in range(n):
                            last = pe.transpose(banks[b // 4 % 2][:, k * GROUPS:(k + 1) * GROUPS],
                                                src_f[:, (b + k) * 128:(b + k + 1) * 128], ident[0:GROUPS, 0:GROUPS])
                        last.then_inc(src_turned, 1)

        dst_mixed = nc.values_load(mixed_i[0:1, 0:1], min_val=0, max_val=1)
        with nc.If(dst_mixed > 0):
            with ExitStack() as stage:
                def tmp(name, shape, dt):
                    return stage.enter_context(nc.sbuf_tensor(name, shape, dt))

                local_e = tmp("local_e", [128, GE], f32)
                row = tmp("scan_row", [128, GE], f32)
                found = tmp("found", [128, GE], f32)
                zero = tmp("zero", [128, (E + TILES * WIN) // 128], f32)
                node = tmp("node", [128, 1], f32)
                group_max = tmp("group_max", [128, 1], f32)
                in_all = tmp("in_all", [128, 1], f32)
                ofs = tmp("ofs", [128, 1], f32)
                last = tmp("last", [128, 1], f32)
                none = tmp("none", [128, 1], f32)
                spot = tmp("spot", [128, 1], i32)
                one = tmp("one", [128, 1], f32)
                with nc.Block() as block:
                    @block.gpsimd
                    def _(pool):
                        pool.iota(local_e[:, :], [[1, GE]], base=1, channel_multiplier=0,
                                  allow_small_or_imprecise_dtypes=True).then_inc(zero_marks, 1)
                        pool.memset(zero[:, :], 0.0).then_inc(zero_marks, 1)
                        pool.memset(one[:, :], 1.0).then_inc(zero_marks, 1)
                        pool.memset(node[:, :], 0.0).then_inc(zero_marks, 1)
                        pool.wait_ge(zero_marks, 4)

                    @block.vector
                    def _(dve):
                        dve.wait_ge(zero_marks, 4)
                        dve.tensor_copy(node[:, :], iota_p[:, :]).then_inc(zero_marks, 1)
                        dve.wait_ge(zero_marks, 5)

                    @block.scalar
                    def _(act):
                        act.wait_ge(zero_marks, 4)

                    @block.tensor
                    def _(pe):
                        pe.wait_ge(zero_marks, 4)

                    @block.sync
                    def _(sp):
                        sp.wait_ge(zero_marks, 4)
                        sp.wait_ge(stored_marks, 16)
                        sp.dma_start(last_marks.rearrange("(p a) o -> p (a o)", p=128), zero[:, :]).then_inc(stored_pad, 16)
                        sp.wait_ge(stored_pad, 16)

                with nc.Fori(0, TILES) as _t:
                    with nc.Block() as block:
                        @block.sync
                        def _(sp):
                            with sp.Fori(0, GROUPS) as g:
                                sp.wait_ge(scan_free, g + 1)
                                sp.dma_start(row[:, :], keys[bass.ds(g, 1), :].to_broadcast([128, GE])).then_inc(scan_in, 16)

                        @block.vector
                        def _(dve):
                            pre = Chain(dve, scan_chain)
                            pre(dve.memset(last[:, :], 0.0))
                            pre(dve.memset(ofs[:, :], 0.0))
                            dve.sem_inc(scan_free, 1)
                            with dve.Fori(0, GROUPS) as g:
                                link = Chain(dve, scan_chain, 5 * g + 2)
                                dve.wait_ge(scan_in, 16 * g + 16)
                                link(dve.scalar_tensor_tensor(found[:, :], row[:, :], node[:, 0:1], local_e[:, :],
                                                              ALU.is_equal, ALU.mult))
                                dve.sem_inc(scan_free, 1)
                                link(dve.tensor_reduce(group_max[:, :], found[:, :], AX, ALU.max))
                                link(dve.tensor_scalar(in_all[:, :], group_max[:, :], 0.0, ofs[:, 0:1], ALU.is_gt, ALU.mult))
                                link(dve.scalar_tensor_tensor(last[:, :], in_all[:, :], group_max[:, 0:1], last[:, :], ALU.add, ALU.max))
                                link(dve.tensor_scalar(ofs[:, :], ofs[:, :], float(GE), None, ALU.add))
                            post = Chain(dve, scan_ready)
                            post(dve.tensor_scalar(none[:, :], last[:, :], 0.0, float(E + 1), ALU.is_equal, ALU.mult))
                            post(dve.tensor_scalar(in_all[:, :], last[:, :], 0.0, node[:, 0:1], ALU.is_equal, ALU.mult))
                            post(dve.tensor_tensor(none[:, :], none[:, :], in_all[:, :], ALU.add))
                            post(dve.scalar_tensor_tensor(none[:, :], last[:, :], -1.0, none[:, :], ALU.add, ALU.add))
                            post(dve.tensor_copy(spot[:, :], none[:, :]))
                            post(dve.tensor_scalar(node[:, :], node[:, :], float(WIN), None, ALU.add))

                        @block.gpsimd
                        def _(pool):
                            pool.wait_ge(scan_ready, 5)
                            pool.indirect_dma_start(last_marks, bass.IndirectOffsetOnAxis(ap=spot[:, 0:1], axis=0), one[:, :], None)\
                                .then_inc(scan_mark, 16)
                            pool.wait_ge(scan_mark, 16)
                    nc.gpsimd.dma_reset(range(scan_mark.num, scan_mark.num + 1))
                    nc.all_engine_barrier(sems_to_clear=of_scan)

        def layer_norm(dve, link, to, of, scratch, vars_before):
            link(dve.tensor_reduce(mean[:, :], of, AX, ALU.add))
            link(dve.tensor_scalar(mean[:, :], mean[:, :], 1.0 / D, None, ALU.mult))
            link(dve.tensor_tensor(to, of, along(mean[:, :], D), ALU.subtract))
            link(dve.tensor_tensor(scratch, to, to, ALU.mult))
            link(dve.tensor_reduce(var[:, :], scratch, AX, ALU.add))
            dve.tensor_scalar(var[:, :], var[:, :], 1.0 / D, EPS, ALU.mult, ALU.add).then_inc(ln_var, 1)
            dve.wait_ge(ln_std, vars_before + 1)
            link(dve.reciprocal(std[:, :], std[:, :]))
            link(dve.tensor_tensor(to, to, along(std[:, :], D), ALU.mult))
            link(dve.tensor_scalar(to, to, 0.0, None, ALU.max))

        def take_root(act, n):
            act.wait_ge(ln_var, n)
            act.activation(std[:, :], var[:, :], ACT.Sqrt).then_inc(ln_std, 1)

        of_layer0 = ctx.enter_context(ExitStack())

        def sb0(name, shape, dt):
            return of_layer0.enter_context(nc.sbuf_tensor(name, shape, dt))

        placeT = sb0("placeT", [128, GROUPS, CD], f32)
        stepT = sb0("stepT", [128, GROUPS, CD], f32)
        columnT = sb0("columnT", [128, GROUPS, CD], f32)
        iota_cols = sb0("iota_cols", [128, HOTC], f16)
        table = sb0("table", [PN, NT, F0], bf16)[:, :, :]
        with ExitStack() as stage:
            near_i = stage.enter_context(nc.sbuf_tensor("near_i", [128, GROUPS, CD], i32))
            over = stage.enter_context(nc.sbuf_tensor("over", [128, GROUPS, CD], f32))
            cols_f = stage.enter_context(nc.sbuf_tensor("cols_f", [128, HOTC], f32))
            type_i = stage.enter_context(nc.sbuf_tensor("type_i", [GROUPS, GE], i32))
            type_b = stage.enter_context(nc.sbuf_tensor("type_b", [GROUPS, GE], bf16))
            h = stage.enter_context(nc.sbuf_tensor("h0", [PN, NT, D], f32))
            scratch = stage.enter_context(nc.sbuf_tensor("scratch0", [PN, NT, D], f32))
            parts = table.rearrange("p t (s d) -> p t s d", d=D)
            with nc.Block() as block:
                @block.gpsimd
                def _(pool):
                    link = Chain(pool, cols_chain)
                    link(pool.iota(cols_f[:, :], [[1, HOTC]], base=0, channel_multiplier=0, allow_small_or_imprecise_dtypes=True))
                    link(pool.tensor_copy(iota_cols[:, :], cols_f[:, :]))
                    pool.wait_ge(stored_marks, 16)
                    link(pool.memset(acc[0:D, :], 0.0))

                @block.scalar
                def _(act):
                    link = Chain(act, guess_chain)
                    link(act.activation(stepT[:, :, :], srcT[:, 0:GROUPS, CG:CH], ACT.Copy, scale=1.0 / NT))
                    link(act.copy(near_i[:, :, :], stepT[:, :, :]))
                    link(act.copy(placeT[:, :, :], near_i[:, :, :]))
                    act.wait_ge(loaded["type"], 16)
                    act.copy(type_b[:, :], type_i[:, :]).then_inc(types_done, 1)
                    take_root(act, 1)

                @block.vector
                def _(dve):
                    link = Chain(dve, ln_chain)
                    layer_norm(dve, link, h[:, :, :], xb[:, :, :], scratch[:, :, :], 0)
                    link(dve.tensor_tensor(h[:, :, :], h[:, :, :], along(cjt[:, :], D), ALU.mult))
                    link(dve.tensor_copy(parts[:, :, 0, :], h[:, :, :]))
                    link(dve.tensor_tensor(h[:, :, :], h[:, :, :], parts[:, :, 0, :], ALU.subtract))
                    link(dve.tensor_copy(parts[:, :, 1, :], h[:, :, :]))
                    link(dve.tensor_tensor(h[:, :, :], h[:, :, :], parts[:, :, 1, :], ALU.subtract))
                    dve.tensor_copy(parts[:, :, 2, :], h[:, :, :]).then_inc(table0_done, 1)
                    link = Chain(dve, split_chain)
                    dve.wait_ge(guess_chain, 3)
                    link(dve.scalar_tensor_tensor(stepT[:, :, :], placeT[:, :, :], -float(NT), srcT[:, 0:GROUPS, CG:CH], ALU.mult, ALU.add))
                    for limit, by in ((0.0, -1.0), (float(NT), 1.0)):
                        link(dve.tensor_scalar(over[:, :, :], stepT[:, :, :], limit, by, ALU.is_lt if by < 0 else ALU.is_ge, ALU.mult))
                        link(dve.tensor_tensor(placeT[:, :, :], placeT[:, :, :], over[:, :, :], ALU.add))
                        link(dve.scalar_tensor_tensor(stepT[:, :, :], over[:, :, :], -float(NT), stepT[:, :, :], ALU.mult, ALU.add))
                    link(dve.tensor_scalar(stepT[:, :, :], stepT[:, :, :], float(SLOTS), None, ALU.mult))

                @block.sync
                def _(sp):
                    sp.dma_start(type_i[:, :], etype.rearrange("(g e) -> g e", e=GE)).then_inc(loaded["type"], 16)
                    sp.wait_ge(types_done, 1)
                    sp.dma_start(type_rows, type_b[:, :]).then_inc(stored_types, 16)
                    sp.wait_ge(table0_done, 1)
                    sp.dma_start(table0.rearrange("(p t) f -> p (t f)", t=NT), table.rearrange("p t f -> p (t f)"))\
                      .then_inc(stored_table0, 16)
                    sp.wait_ge(stored_types, 16)

        def prepare_pass(p, layer):
            with ExitStack() as stage:
                def tmp(name, shape, dt):
                    return stage.enter_context(nc.sbuf_tensor(name + str(layer), shape, dt))

                left = tmp("left", [GROUPS, GE], f32)
                key = tmp("key", [GROUPS, GE], f32)
                key_b = tmp("key_b", [GROUPS, GE], bf16)
                slot = tmp("slot", [GROUPS, GE], f32)
                least = tmp("least", [GROUPS, QC * QR], f32)
                nodes = tmp("nodes", [GROUPS, 2, QR, QC, SLOTS], f32)
                with nc.Block() as block:
                    @block.gpsimd
                    def _(pool):
                        pool.wait_ge(left_out, 16)

                    @block.sync
                    def _(sp):
                        version = (p + 127) // 128 * GROUPS
                        sp.dma_start(left[:, :], keys[bass.ds(version, GROUPS), :]).then_inc(keys_in, 16)
                        sp.wait_ge(key_rounded, 1)
                        sp.dma_start(key_rows, key_b[:, :]).then_inc(key_rows_out, 16)
                        sp.wait_ge(left_done, 1)
                        sp.dma_start(keys[GROUPS:2 * GROUPS, :], left[:, :]).then_inc(left_out, 16)
                        sp.wait_ge(key_rows_out, 16)
                        sp.wait_ge(left_out, 16)

                    @block.vector
                    def _(dve):
                        link = Chain(dve, prep_link)
                        chunks = key[:, :].rearrange("g (k e) -> g k e", e=128)
                        by_set = (least[:, :].rearrange("g (q c) -> g q c", q=QR) if layer == 0
                                  else least[:, :].rearrange("g (c q) -> g q c", q=QR))
                        link(dve.memset(least[:, CH:QC * QR], -1000.0))
                        dve.wait_ge(keys_in, 16)
                        link(dve.tensor_reduce(base_col[0:GROUPS, :], left[:, :], AX, ALU.min))
                        link(dve.tensor_scalar(base_col[0:GROUPS, :], base_col[0:GROUPS, :], float(N - 1), None, ALU.min))
                        link(dve.tensor_scalar(key[:, :], left[:, :], base_col[0:GROUPS, 0:1], None, ALU.subtract))
                        link(dve.tensor_reduce(least[:, 0:CH], chunks, AX, ALU.min))
                        link(dve.tensor_scalar(least[:, 0:CH], least[:, 0:CH], 255.0, None, ALU.min))
                        dve.tensor_tensor(slot[:, :].rearrange("g (k e) -> g k e", e=128), chunks, along(least[:, 0:CH], 128),
                                          ALU.subtract).then_inc(slots_made, 1)
                        for way, of in enumerate((least[:, :].rearrange("g (q c) -> g q c", q=QR),
                                                  least[:, :].rearrange("g (c q) -> g q c", q=QR))):
                            dve.tensor_tensor(nodes[:, way, :, :, :], of.unsqueeze(3).to_broadcast([GROUPS, QR, QC, SLOTS]),
                                              iota_r[0:GROUPS, 0:SLOTS].unsqueeze(1).unsqueeze(1).to_broadcast([GROUPS, QR, QC, SLOTS]),
                                              ALU.add).then_inc(nodes_made, 1)
                        dve.wait_ge(key_rounded, 1)
                        link(dve.tensor_scalar(key[:, :], key[:, :], float(WIN), None, ALU.is_lt))
                        link(dve.scalar_tensor_tensor(key[:, :], slot[:, :], float(SLOTS), key[:, :], ALU.is_lt, ALU.mult))
                        dve.scalar_tensor_tensor(left[:, :], key[:, :], BIG, left[:, :], ALU.mult, ALU.add).then_inc(left_done, 1)
                        dve.wait_ge(left_done, 1)
                        dve.tensor_reduce(left_col[0:GROUPS, :], left[:, :], AX, ALU.min).then_inc(cols_made, 1)
                        dve.wait_ge(prep_turned, 1)
                        link(dve.tensor_copy(base_f[:, 1:GROUPS + 1], banks[2][0:1, 0:GROUPS]))
                        link(dve.tensor_copy(base_i[:, :], base_f[:, :]))
                        link(dve.tensor_reduce(more[:, :], banks[2][0:1, 128:128 + GROUPS], AX, ALU.min))
                        link(dve.tensor_scalar(more[:, :], more[:, :], BIG / 2, None, ALU.is_lt))
                        link(dve.tensor_tensor(passes_f[:, :], passes_f[:, :], more[:, :], ALU.add))
                        link(dve.tensor_copy(passes_i[:, :], passes_f[:, :]))
                        if layer == 0:
                            mine = slotT[:, :, CG:CH]
                            dve.wait_ge(slots_copied, -(-CH // 4))
                            link(dve.tensor_scalar(columnT[:, :, :], mine, float(SLOTS), BIG, ALU.is_ge, ALU.mult))
                            link(dve.tensor_tensor(columnT[:, :, :], columnT[:, :, :], mine, ALU.add))
                            link(dve.tensor_tensor(columnT[:, :, :], columnT[:, :, :], stepT[:, :, :], ALU.add))

                    @block.tensor
                    def _(pe):
                        pe.wait_ge(slots_made, 1)
                        for b in range(0, CH, 4):
                            n = min(4, CH - b)
                            if b >= 8:
                                pe.wait_ge(slots_copied, b // 4 - 1)
                            for k in range(n):
                                last = pe.transpose(banks[b // 4 % 2][:, k * GROUPS:(k + 1) * GROUPS],
                                                    slot[:, (b + k) * 128:(b + k + 1) * 128], ident[0:GROUPS, 0:GROUPS])
                            last.then_inc(slots_turned, 1)
                        pe.wait_ge(nodes_made, 2)
                        for way in range(2):
                            for q in range(QR):
                                last = pe.transpose(banks[3 + way][0:QS, q * GROUPS:(q + 1) * GROUPS],
                                                    nodes[:, way, q, :, :].rearrange("g c s -> g (c s)"), ident[0:GROUPS, 0:GROUPS])
                            last.then_inc(nodes_turned, 1)
                        pe.wait_ge(cols_made, 1)
                        pe.transpose(banks[2][0:1, 0:GROUPS], base_col[0:GROUPS, :], ident[0:GROUPS, 0:GROUPS])
                        pe.transpose(banks[2][0:1, 128:128 + GROUPS], left_col[0:GROUPS, :], ident[0:GROUPS, 0:GROUPS])\
                          .then_inc(prep_turned, 1)

                    @block.scalar
                    def _(act):
                        act.wait_ge(prep_link, 4)
                        act.copy(key_b[:, :], key[:, :]).then_inc(key_rounded, 1)
                        for b in range(0, CH, 4):
                            n = min(4, CH - b)
                            act.wait_ge(slots_turned, b // 4 + 1)
                            act.copy(slotT[:, :, b:b + n].rearrange("p g k -> p k g"),
                                     banks[b // 4 % 2][:, 0:n * GROUPS].rearrange("p (k g) -> p k g", g=GROUPS))\
                               .then_inc(slots_copied, 1)
                        for way in range(2):
                            act.wait_ge(nodes_turned, way + 1)
                            act.copy(nodeT[:, way, :, 1:GROUPS + 1],
                                     banks[3 + way][0:QS, 0:QR * GROUPS].rearrange("s (q g) -> s q g", g=GROUPS)).then_inc(nodes_copied, 1)
                        act.wait_ge(nodes_copied, 2)
            nc.regs_load(passes_end, passes_i[0:1, 0:1])

        def close_pass():
            nc.gpsimd.dma_reset(of_gathers)
            nc.all_engine_barrier(sems_to_clear=of_pass)

        def gather(pool, rows, idx, table, units):
            with pool.Fori(0, GROUPS) as g:
                for u in range(len(units)):
                    pool.wait_ge(idx_ready, len(units) * g + u + 1)
                    pool.wait_ge(slot_free, len(units) * g + u + 1)
                    pool.sem_inc(pool_turn, 1)
                    for k in range(units[u]):
                        pool.indirect_dma_start(rows[:, u, k, :], None, table,
                                                bass.IndirectOffsetOnAxis(ap=idx[:, u, k:k + 1], axis=0))\
                            .then_inc(gathered[u], 16)

        def window(eng, entry):
            return eng.value_load(base_i[0:1, bass.ds(entry, 1)], min_val=0, max_val=N - 1)

        def next_indices(dve, idx, g, u, c, n):
            dve.tensor_copy(idx[:, u, 0:n], srcT[:, bass.ds(g, 1), c:c + n].squeeze(1)).then_inc(idx_ready, 1)

        def slots_of(g, c, n):
            return (along(slotT[:, bass.ds(g, 1), c:c + n].squeeze(1), SLOTS),
                    iota_r[:, 0:SLOTS].unsqueeze(1).to_broadcast([128, n, SLOTS]))

        def place_nodes(dve, node_hot, layer, entry):
            dve.tensor_tensor(node_hot[:, :, :], along(nodeT[:, layer, :, bass.ds(entry, 1)].rearrange("s q g -> s (q g)"), WIN),
                              iota_r[0:QS, :].unsqueeze(1).to_broadcast([QS, QR, WIN]), ALU.is_equal).then_inc(nodes_hot, 1)

        def place_sums(pe, slot_sums, node_hot, n):
            pe.wait_ge(nodes_hot, n)
            pe.wait_ge(slot_sums_copied, n)
            pe.wait_ge(sums_free, n)
            pe.sem_inc(pe_turn, 1)
            for q in range(QR):
                last = pe.matmul(banks[7][0:D, 0:WIN], slot_sums[:, q, :], node_hot[:, q, :], start=(q == 0), stop=(q == QR - 1))
            last.then_inc(sums_ready, 1)

        def add_window(dve, entry, n):
            at = window(dve, entry)
            dve.wait_ge(sums_ready, n)
            dve.wait_ge(sums_free, n)
            dve.tensor_tensor(acc[0:D, bass.ds(at, WIN)], acc[0:D, bass.ds(at, WIN)], banks[7][0:D, 0:WIN], ALU.add)\
               .then_inc(sums_free, 1)

        def two_by_two(engine, group):
            with engine.Fori(0, GROUPS // 2) as i:
                group(2 * i, 0, False)
                group(2 * i + 1, 1, False)
            group(GROUPS - 1, 0, True)

        nc.regs_mov(passes_end, 1)
        with nc.Fori(0, passes_end) as p:
            prepare_pass(p, 0)
            with ExitStack() as stage:
                def tmp(name, shape, dt):
                    return stage.enter_context(nc.sbuf_tensor(name, shape, dt))

                HOTS = max(h for h in (2, 3, 4) if 2 * CD % h == 0)
                rows = tmp("rows0", [128, GUNITS, GUC, F0], bf16)
                idx = tmp("idx0", [128, GUNITS, GUC], i32)
                hot = tmp("hot0", [128, GUNITS, GUC, SLOTS], bf16)
                place_hot = tmp("place_hot", [128, HOTS, PN], bf16)
                column_hot = tmp("column_hot", [128, HOTS, HOTC], bf16)
                counts = tmp("counts", [PN, 2, NT, CD, SLOTS], bf16)
                parts_sb = tmp("parts_sb", [F0, QR * QS], f32)
                slot_sums = tmp("slot_sums0", [QS, QR, D], f32)
                node_hot = tmp("node_hot0", [QS, QR, WIN], f32)
                count_pairs, gathered_bank, slot_bank, counted_bank = pairs[0:2], banks[4], banks[5], banks[6]

                def copies(by, g, j):
                    if j < 0:
                        return copies(by, g - 1, j + CD)
                    return len(by) * (g + 1) + sum(i <= j for i in by)

                def copy_counts(engine, copy, done, g, half, j):
                    engine.wait_ge(counts_made, CD * g + j + 1 + HOTS)
                    engine.wait_ge(counted_summed, g + 1)
                    copy(counts[:, half, :, j, :].rearrange("p (b t) s -> p b t s", b=2),
                         count_pairs[turn_of(half, j) % 2][0:PN, :, 0:HOTC // 2].rearrange("p b (t s) -> p b t s", s=SLOTS))\
                        .then_inc(done, 1)

                def turn_of(half, j):
                    return CD * half + j

                units = [min(GUC, CG - u * GUC) for u in range(GUNITS)]
                AHEAD = 2

                def turn_of_unit(u):
                    return (u + 1) * (CD - 1) // GUNITS

                with nc.Block() as block:
                    @block.gpsimd
                    def _(pool):
                        pool.wait_ge(stored_table0, 16)
                        gather(pool, rows, idx, table0, units)

                    @block.scalar
                    def _(act):
                        def copy_parts(n):
                            act.wait_ge(slot_free, GUNITS * n)
                            act.wait_ge(counted_summed, n + 1)
                            act.copy(parts_sb[:, 0:CG * SLOTS], gathered_bank[0:F0, 0:CG * SLOTS]).then_inc(part_copied, 1)
                            act.copy(parts_sb[:, CG * SLOTS:CH * SLOTS], counted_bank[0:F0, 0:CD * SLOTS]).then_inc(part_copied, 1)

                        def copy_slot_sums(n):
                            act.wait_ge(slot_sums_made, n)
                            act.copy(slot_sums[:, :, :], slot_bank[0:QS, 0:QR * D].rearrange("s (q d) -> s q d", d=D))\
                               .then_inc(slot_sums_copied, 1)

                        act.sem_inc(counts_by_act, len(BY_ACT))
                        for j in BY_ACT:
                            copy_counts(act, act.copy, counts_by_act, 0, 0, j)
                        act.wait_ge(bank_zero, 2)

                        def group(g, half, last):
                            for j in range(CD):
                                if j in BY_ACT and not last:
                                    copy_counts(act, act.copy, counts_by_act, g + 1, 1 - half, j)
                                if j == 0:
                                    copy_parts(g + 1)
                                if j == 5:
                                    copy_slot_sums(g + 1)

                        two_by_two(act, group)
                        copy_parts(GROUPS + 1)
                        copy_slot_sums(GROUPS + 1)

                    @block.vector
                    def _(dve):
                        def hot_columns(g, half, j):
                            slot = turn_of(half, j) % HOTS
                            dve.wait_ge(counts_made, CD * g + j + 1)
                            dve.tensor_scalar(place_hot[:, slot, :], iota_cols[:, 0:PN],
                                              placeT[:, bass.ds(g, 1), j:j + 1].squeeze(1), None, ALU.is_equal).then_inc(columns_ready, 1)
                            dve.tensor_scalar(column_hot[:, slot, :], iota_cols[:, :],
                                              columnT[:, bass.ds(g, 1), j:j + 1].squeeze(1), None, ALU.is_equal).then_inc(columns_ready, 1)

                        pre = Chain(dve, dve_chain)
                        dve.memset(gathered_bank[0:F0, 0:CG * SLOTS], 0.0).then_inc(bank_zero, 1)
                        dve.memset(counted_bank[0:F0, 0:CD * SLOTS], 0.0).then_inc(bank_zero, 1)
                        pre(dve.memset(parts_sb[:, :], 0.0))
                        dve.sem_inc(sums_free, 1)
                        for u in range(GUNITS):
                            next_indices(dve, idx, 0, u, u * GUC, units[u])
                        dve.sem_inc(counts_by_dve, len(BY_DVE))
                        for j in range(CD):
                            hot_columns(0, 0, j)
                            if j - 2 in BY_DVE:
                                copy_counts(dve, dve.tensor_copy, counts_by_dve, 0, 0, j - 2)

                        def group(g, half, last):
                            for j in range(CD):
                                if not last:
                                    hot_columns(g + 1, 1 - half, j)
                                if j - 2 in BY_DVE and not last:
                                    copy_counts(dve, dve.tensor_copy, counts_by_dve, g + 1, 1 - half, j - 2)
                                for u in range(GUNITS):
                                    if j == min(turn_of_unit(u) + 1, CD - 1):
                                        dve.wait_ge(gathered[u], 16 * units[u] * g + 16 * units[u])
                                        next_indices(dve, idx, g + 1, u, u * GUC, units[u])
                                    if j != turn_of_unit(u - 1):
                                        continue
                                    dve.wait_ge(slot_free, GUNITS * g + u + 1)
                                    mine, each = slots_of(g, u * GUC, units[u])
                                    dve.tensor_tensor(hot[:, u, 0:units[u], :], mine, each, ALU.is_equal).then_inc(hot_ready, 1)
                                if j == 3:
                                    place_nodes(dve, node_hot, 0, g)
                                if j == 10:
                                    add_window(dve, g, g + 1)

                        two_by_two(dve, group)
                        place_nodes(dve, node_hot, 0, GROUPS)
                        add_window(dve, GROUPS, GROUPS + 1)
                        dve.wait_ge(sums_free, GROUPS + 2)

                    @block.tensor
                    def _(pe):
                        def count(g, half, j):
                            slot, pair = turn_of(half, j) % HOTS, count_pairs[turn_of(half, j) % 2]
                            pe.wait_ge(columns_ready, 2 * CD * g + 2 * j + 2)
                            if (j - 2) % CD in BY_ACT:
                                pe.wait_ge(counts_by_act, copies(BY_ACT, g, j - 2))
                            else:
                                pe.wait_ge(counts_by_dve, copies(BY_DVE, g, j - 2))
                            for b in range(2):
                                last = pe.matmul(pair[0:PN, b, 0:HOTC // 2], place_hot[:, slot, :],
                                                 column_hot[:, slot, b * (HOTC // 2):(b + 1) * (HOTC // 2)], start=True, stop=True)
                            last.then_inc(counts_made, 1)

                        def sum_counted(g, half, ts):
                            if ts[0] == 0:
                                pe.wait_ge(counts_by_act, copies(BY_ACT, g, CD - 1))
                                pe.wait_ge(counts_by_dve, copies(BY_DVE, g, CD - 1))
                            for t in ts:
                                last = pe.matmul(counted_bank[0:F0, 0:CD * SLOTS], table[:, t, :],
                                                 counts[:, half, t, :, :].rearrange("p c s -> p (c s)"),
                                                 start=(t == 0), stop=(t == NT - 1))
                            if ts[-1] == NT - 1:
                                last.then_inc(counted_summed, 1)

                        def sum_gathered(g, u):
                            pe.wait_ge(hot_ready, GUNITS * g + u + 1)
                            pe.wait_ge(gathered[u], 16 * units[u] * g + 16 * units[u])
                            for k in range(units[u]):
                                c = u * GUC + k
                                last = pe.matmul(gathered_bank[0:F0, c * SLOTS:(c + 1) * SLOTS], rows[:, u, k, :], hot[:, u, k, :],
                                                 start=True, stop=True)
                            last.then_inc(slot_free, 1)

                        def add_parts(n):
                            pe.wait_ge(part_copied, 2 * n)
                            for q in range(QR):
                                last = pe.matmul(slot_bank[0:QS, q * D:(q + 1) * D], parts_sb[:, q * QS:(q + 1) * QS], sum_w[:, :],
                                                 start=True, stop=True)
                            last.then_inc(slot_sums_made, 1)

                        pe.sem_inc(slot_free, GUNITS)
                        pe.sem_inc(counts_made, HOTS)
                        pe.sem_inc(counted_summed, 2)
                        for j in range(CD):
                            count(0, 0, j)

                        def group(g, half, last):
                            steps = CD - AHEAD
                            for j in range(CD):
                                if not last:
                                    count(g + 1, 1 - half, j)
                                if j == AHEAD:
                                    pe.wait_ge(part_copied, 2 * g + 2)
                                if j >= AHEAD:
                                    sum_counted(g, half, range((j - AHEAD) * NT // steps, (j - AHEAD + 1) * NT // steps))
                                for u in range(GUNITS):
                                    if j == turn_of_unit(u):
                                        sum_gathered(g, u)
                                if j == 4:
                                    add_parts(g + 1)
                                if j == 7:
                                    place_sums(pe, slot_sums, node_hot, g + 1)

                        two_by_two(pe, group)
                        add_parts(GROUPS + 1)
                        place_sums(pe, slot_sums, node_hot, GROUPS + 1)
            close_pass()

        of_layer0.close()
        nc.regs_load(prepare_again, passes_i[0:1, 0:1])

        lastT = sb("lastT", [128, GROUPS, CH], f32)
        with ExitStack() as stage:
            def tmp(name, shape, dt):
                return stage.enter_context(nc.sbuf_tensor(name, shape, dt))

            rows1 = tmp("rows1", [PN, NT, 2 * D], f32)
            row_y = tmp("row_y", [PN, NT, D], f32)
            agg = tmp("agg", [PN, NT, D], f32)
            h_turned_sb = tmp("h_turned_sb", [128, 2, PN], f32)
            with nc.sbuf_tensor("marks_again", [GROUPS, GE], f32) as marks, nc.Block() as block:
                per = 16
                batches = [(b, min(per, NT - b)) for b in range(0, NT, per)]

                @block.tensor
                def _(pe):
                    for i, (b, n) in enumerate(batches):
                        if i >= 2:
                            pe.wait_ge(agg_taken, i - 1)
                        for t in range(n):
                            last = pe.transpose(banks[i % 2][0:PN, t * D:(t + 1) * D],
                                                acc[0:D, b + t:b + t + (PN - 1) * NT + 1:NT], ident[0:D, 0:D])
                        last.then_inc(agg_made, 1)
                    pe.wait_ge(marks_in, 16)
                    for b in range(0, CH, 4):
                        n = min(4, CH - b)
                        if b >= 8:
                            pe.wait_ge(marks_copied, b // 4 - 1)
                        for k in range(n):
                            last = pe.transpose(banks[2 + b // 4 % 2][:, k * GROUPS:(k + 1) * GROUPS],
                                                marks[:, (b + k) * 128:(b + k + 1) * 128], ident[0:GROUPS, 0:GROUPS])
                        last.then_inc(marks_turned, 1)

                @block.sync
                def _(sp):
                    sp.dma_start(marks[:, :], last_marks[0:E, :].rearrange("(g e) o -> g (e o)", e=GE)).then_inc(marks_in, 16)
                    sp.wait_ge(marks_in, 16)

                @block.vector
                def _(dve):
                    link = Chain(dve, mid_chain)
                    for i, (b, n) in enumerate(batches):
                        dve.wait_ge(agg_made, i + 1)
                        made = banks[i % 2][0:PN, 0:n * D].rearrange("p (t c) -> p t c", c=D)
                        dve.tensor_tensor(agg[:, b:b + n, :], made, along(cit[:, b:b + n], D), ALU.mult).then_inc(agg_taken, 1)
                    dve.wait_ge(agg_taken, len(batches))
                    link(dve.tensor_tensor(xb[:, :, :], xb[:, :, :], agg[:, :, :], ALU.add))
                    layer_norm(dve, link, rows1[:, :, 0:D], xb[:, :, :], agg[:, :, :], 1)
                    link(dve.memset(passes_f[:, :], 1.0))

                @block.scalar
                def _(act):
                    for b in range(0, CH, 4):
                        n = min(4, CH - b)
                        act.wait_ge(marks_turned, b // 4 + 1)
                        act.copy(lastT[:, :, b:b + n].rearrange("p g k -> p k g"),
                                 banks[2 + b // 4 % 2][:, 0:n * GROUPS].rearrange("p (k g) -> p k g", g=GROUPS))\
                           .then_inc(marks_copied, 1)
                    take_root(act, 2)

            with nc.Block() as block:
                quads = NT // 4

                @block.gpsimd
                def _(pool):
                    pool.memset(acc[0:D, :], 0.0).then_inc(restart, 1)
                    pool.wait_ge(restart, 1)

                @block.tensor
                def _(pe):
                    def turn(i):
                        if i >= 2:
                            pe.wait_ge(h_copied, i - 1)
                        pe.transpose(banks[i % 2][:, 0:PN], agg[:, 4 * i:4 * i + 4, :].rearrange("p t d -> p (t d)"),
                                     ident[0:PN, 0:PN]).then_inc(h_turned, 1)

                    pe.wait_ge(h_done, 1)
                    turn(0)
                    for i in range(quads):
                        if i + 1 < quads:
                            turn(i + 1)
                        pe.wait_ge(h_copied, i + 1)
                        if i >= 2:
                            pe.wait_ge(a_taken, 2 * i - 2)
                        pe.matmul(banks[2 + i % 2][0:PN, 0:8 * D], h_turned_sb[:, i % 2, :], both_a[:, :, :].rearrange("p q a -> p (q a)"),
                                  start=True, stop=True).then_inc(a_made, 1)

                @block.scalar
                def _(act):
                    for i in range(quads):
                        act.wait_ge(h_turned, i + 1)
                        if i >= 2:
                            act.wait_ge(a_made, i - 1)
                        act.copy(h_turned_sb[:, i % 2, :], banks[i % 2][:, 0:PN]).then_inc(h_copied, 1)

                @block.vector
                def _(dve):
                    dve.tensor_copy(agg[:, :, :], rows1[:, :, 0:D]).then_inc(h_done, 1)
                    for i in range(quads):
                        dve.wait_ge(a_made, i + 1)
                        made = banks[2 + i % 2][0:PN, 0:8 * D].rearrange("p (t c) -> p t c", c=2 * D)
                        dve.tensor_tensor(rows1[:, 4 * i:4 * i + 4, D:2 * D], made[:, :, 0:D],
                                          b1_row[0:PN, :].unsqueeze(1).to_broadcast([PN, 4, D]), ALU.add).then_inc(a_taken, 1)
                        dve.tensor_copy(row_y[:, 4 * i:4 * i + 4, :], made[:, :, D:2 * D]).then_inc(a_taken, 1)
                    dve.wait_ge(a_taken, 2 * quads)

            parts = tmp("parts1", [PN, NT, 3, D], bf16)
            zeros = tmp("zeros", [WIN, 3 * D], bf16)
            with nc.Block() as block:
                @block.vector
                def _(dve):
                    link = Chain(dve, tables_done)
                    link(dve.memset(zeros[:, :], 0.0))
                    link(dve.tensor_copy(parts[:, :, 0, :], row_y[:, :, :]))
                    link(dve.tensor_tensor(row_y[:, :, :], row_y[:, :, :], parts[:, :, 0, :], ALU.subtract))
                    link(dve.tensor_copy(parts[:, :, 1, :], row_y[:, :, :]))
                    link(dve.tensor_tensor(row_y[:, :, :], row_y[:, :, :], parts[:, :, 1, :], ALU.subtract))
                    link(dve.tensor_copy(parts[:, :, 2, :], row_y[:, :, :]))

                @block.sync
                def _(sp):
                    sp.dma_start(table1.rearrange("(p t) f -> p (t f)", t=NT),
                                 rows1[:, :, :].rearrange("p t d -> p (t d)")).then_inc(stored, 16)
                    sp.wait_ge(tables_done, 6)
                    sp.dma_start(dst_table[0:N, :].rearrange("(p t) f -> p (t f)", t=NT),
                                 parts[:, :, :, :].rearrange("p t s d -> p (t s d)")).then_inc(stored, 16)
                    sp.dma_start(dst_table[N:NPAD, :], zeros[:, :]).then_inc(stored, 16)
                    sp.wait_ge(stored, 48)

        nc.regs_mov(passes_end, 1)
        with nc.Fori(0, passes_end) as p:
            with nc.If_ne(prepare_again, 1):
                prepare_pass(p, 1)
            nc.regs_mov(prepare_again, 2)
            with ExitStack() as stage:
                def tmp(name, shape, dt):
                    return stage.enter_context(nc.sbuf_tensor(name, shape, dt))

                RING = 3
                rows = tmp("rows_in1", [128, UNITS, UC, 2 * D], f32)
                idx = tmp("idx1", [128, UNITS, UC], i32)
                key_r = tmp("key_r1", [128, UNITS, UE], bf16)
                type_r = tmp("type_r1", [R, UNITS, UE], bf16)
                dst_hot = tmp("dst_hot", [128, RING, UE], bf16)
                type_hot = tmp("type_hot", [R, RING, UE], bf16)
                slot_hot = tmp("slot_hot", [128, UC, SLOTS], f32)
                prod = tmp("prod", [128, UC, D], f32)
                score = tmp("score", [128, 2, UC], f32)
                att = tmp("att", [128, 2, UC], f32)
                factors = tmp("factors", [128, UC, CC], f32)
                by_slot = tmp("by_slot", [128, RING, UC, SLOTS, CC], f32)
                win_raw = tmp("win_raw", [128, 3, D], bf16)
                win = tmp("win", [128, 3, D], bf16)
                sums_sb = tmp("sums_sb", [128, QC, ZC], f32)
                slot_sums = tmp("slot_sums1", [QS, QR, D], f32)
                node_hot = tmp("node_hot1", [QS, QR, WIN], f32)
                y_banks, sum_banks, slot_bank = banks[0:3], banks[3:6], banks[6]

                def before(u):
                    return {0: 2, 1: 2, 2: UNITS}.get(u, RING)

                assert UNITS == 5 and RING == 3 and QC == 2 * ZB + 1 and CH == QR * (QC - 1) + 1
                with nc.Block() as block:
                    @block.gpsimd
                    def _(pool):
                        gather(pool, rows, idx, table1, [UC] * UNITS)

                    @block.sync
                    def _(sp):
                        with sp.Fori(0, GROUPS) as g:
                            at = window(sp, g + 1)
                            sp.wait_ge(win_free, g + 1)
                            sp.dma_start(win_raw[:, :, :], dst_table[bass.ds(at, WIN), :].rearrange("p (s c) -> p s c", c=D))\
                              .then_inc(win_in, 16)
                            for u in range(UNITS):
                                sp.wait_ge(rows_free, 2 * UNITS * g + 2 * u + 2)
                                sp.dma_start(key_r[:, u, :], key_rows[bass.ds(g, 1), u * UE:(u + 1) * UE].to_broadcast([128, UE]))\
                                  .then_inc(key_in[u], 16)
                                sp.dma_start(type_r[:, u, :], type_rows[bass.ds(g, 1), u * UE:(u + 1) * UE].to_broadcast([R, UE]))\
                                  .then_inc(type_in[u], 16)

                    @block.scalar
                    def _(act):
                        def copy_slot_sums(n):
                            act.wait_ge(slot_sums_made, n)
                            act.copy(slot_sums[:, :, :], slot_bank[0:QS, 0:QR * D].rearrange("s (q d) -> s q d", d=D))\
                               .then_inc(slot_sums_copied, 1)

                        def copy_sums(b, parts, blocks):
                            act.copy(sums_sb[0:parts, b * ZB:b * ZB + blocks, :],
                                     sum_banks[b][0:parts, 0:blocks * ZC].rearrange("p (c z) -> p c z", z=ZC)).then_inc(part_copied, 1)

                        act.sem_inc(win_free, 1)
                        act.sem_inc(part_copied, 3)
                        with act.Fori(0, GROUPS) as g:
                            act.wait_ge(win_in, 16 * g + 16)
                            act.wait_ge(y_ready, UNITS * g + UNITS)
                            act.copy(win[:, :, :], win_raw[:, :, :]).then_inc(win_free, 1)
                            for u in range(UNITS):
                                act.wait_ge(score_ready, UNITS * g + u + 1)
                                act.activation(att[:, u % 2, :], score[:, u % 2, :], ACT.Tanh, scale=float(D) ** -0.5)\
                                   .then_inc(att_ready, 1)
                                if u == 2:
                                    copy_slot_sums(g + 1)
                                if u == 3:
                                    act.wait_ge(slot_free, UNITS * g + 3 + UNITS)
                                    copy_sums(0, 128, ZB)
                            act.wait_ge(slot_free, UNITS * g + 2 * UNITS)
                            copy_sums(1, 128, ZB)
                            copy_sums(2, D, 1)
                        copy_slot_sums(GROUPS + 1)

                    @block.vector
                    def _(dve):
                        pre = Chain(dve, dve_chain)
                        pre(dve.memset(sums_sb[:, :, :], 0.0))
                        dve.sem_inc(rows_free, 2 * UNITS)
                        dve.sem_inc(y_free, UNITS)
                        dve.sem_inc(sums_free, 1)
                        for u in range(UNITS):
                            next_indices(dve, idx, 0, u, u * UC, UC)

                        with dve.Fori(0, GROUPS) as g:
                            link = Chain(dve, dve_chain, 2 * UNITS * g + 1)

                            def hot_rows(u):
                                dve.wait_ge(y_ready, UNITS * g + u - before(u) + 1 + UNITS)
                                dve.wait_ge(key_in[u], 16 * g + 16)
                                dve.tensor_scalar(dst_hot[:, u % RING, :], key_r[:, u, :], iota_p[:, 0:1], None, ALU.is_equal)\
                                   .then_inc(rows_free, 1)
                                dve.wait_ge(type_in[u], 16 * g + 16)
                                dve.tensor_scalar(type_hot[:, u % RING, :], type_r[:, u, :], iota_p[0:R, 0:1], None, ALU.is_equal)\
                                   .then_inc(rows_free, 1)

                            hot_rows(0)
                            for u in range(UNITS):
                                if u + 1 < UNITS:
                                    hot_rows(u + 1)
                                r, y = u % RING, y_banks[u % RING][:, 0:UC * YC].rearrange("p (k c) -> p k c", c=YC)
                                dve.wait_ge(y_ready, UNITS * g + u + 1 + UNITS)
                                dve.wait_ge(gathered[u], 16 * UC * g + 16 * UC)
                                link(dve.tensor_tensor(prod[:, :, :], rows[:, u, :, D:2 * D], y[:, :, 0:D], ALU.mult))
                                link(dve.tensor_reduce(score[:, u % 2, :], prod[:, :, :], AX, ALU.add))
                                dve.tensor_scalar(score[:, u % 2, :], score[:, u % 2, :], 0.0, None, ALU.max).then_inc(score_ready, 1)
                                mine, each = slots_of(g, u * UC, UC)
                                dve.tensor_tensor(slot_hot[:, :, :], mine, each, ALU.is_equal)
                                dve.tensor_copy(factors[:, :, NB], lastT[:, bass.ds(g, 1), u * UC:(u + 1) * UC].squeeze(1))
                                dve.wait_ge(att_ready, UNITS * g + u + 1)
                                dve.tensor_tensor(factors[:, :, 0:NB], y[:, :, D:D + NB], along(att[:, u % 2, :], NB), ALU.mult)\
                                   .then_inc(y_free, 1)
                                dve.wait_ge(y_free, UNITS * g + u + 1 + UNITS)
                                dve.wait_ge(slot_free, UNITS * g + u - before(u) + 1 + UNITS)
                                dve.tensor_tensor(by_slot[:, r, :, :, :], slot_hot[:, :, :].unsqueeze(3).to_broadcast([128, UC, SLOTS, CC]),
                                                  factors[:, :, :].unsqueeze(2).to_broadcast([128, UC, SLOTS, CC]), ALU.mult)\
                                   .then_inc(factors_ready, 1)
                                next_indices(dve, idx, g + 1, u, u * UC, UC)
                                dve.wait_ge(idx_ready, UNITS * g + u + 1 + UNITS)
                                if u == 1:
                                    place_nodes(dve, node_hot, 1, g)
                                if u == 3:
                                    add_window(dve, g, g + 1)
                        place_nodes(dve, node_hot, 1, GROUPS)
                        add_window(dve, GROUPS, GROUPS + 1)
                        dve.wait_ge(sums_free, GROUPS + 2)

                    @block.tensor
                    def _(pe):
                        def look_up(g, u):
                            pe.wait_ge(rows_free, 2 * UNITS * g + 2 * u + 2 + 2 * UNITS)
                            pe.wait_ge(y_free, UNITS * g + u - before(u) + 1 + UNITS)
                            for k in range(UC):
                                y, edges = y_banks[u % RING][:, k * YC:(k + 1) * YC], slice(k * 128, (k + 1) * 128)
                                for n in range(3):
                                    pe.matmul(y, type_hot[:, u % RING, edges], type_tabs[:, n, :], start=(n == 0), stop=False)
                                for n in range(3):
                                    last = pe.matmul(y[:, 0:D], dst_hot[:, u % RING, edges], win[:, n, :], start=False, stop=(n == 2))
                            last.then_inc(y_ready, 1)

                        def sum_by_slot(g, u):
                            pe.wait_ge(gathered[u], 16 * UC * g + 16 * UC)
                            pe.wait_ge(factors_ready, UNITS * g + u + 1)
                            for k in range(UC):
                                c = u * UC + k
                                q, b = c % QR, c // QR
                                if c % (QR * ZB) == 0:
                                    pe.wait_ge(part_copied, 3 * g + 1 + b // ZB)
                                last = pe.matmul(sum_banks[b // ZB][q * D:(q + 1) * D, b % ZB * ZC:(b % ZB + 1) * ZC],
                                                 rows[:, u, k, 0:D], by_slot[:, u % RING, k, :, :].rearrange("p s c -> p (s c)"),
                                                 start=True, stop=True)
                            last.then_inc(slot_free, 1)

                        def weigh(n):
                            pe.wait_ge(part_copied, 3 * n)
                            every = sums_sb[:, :, :].rearrange("p c (s f) -> p (c s) f", f=CC)
                            for f in range(CC):
                                last = pe.matmul(slot_bank[0:QS, 0:QR * D], every[:, :, f], w_diag[:, f, :, :].rearrange("p q o -> p (q o)"),
                                                 start=(f == 0), stop=(f == CC - 1))
                            last.then_inc(slot_sums_made, 1)

                        pe.sem_inc(y_ready, UNITS)
                        pe.sem_inc(slot_free, UNITS)
                        with pe.Fori(0, GROUPS) as g:
                            pe.wait_ge(win_free, g + 2)
                            for u in range(UNITS):
                                look_up(g, u)
                                if u >= 1:
                                    sum_by_slot(g, u - 1)
                                if u == 1:
                                    weigh(g + 1)
                                if u == 3:
                                    place_sums(pe, slot_sums, node_hot, g + 1)
                            sum_by_slot(g, UNITS - 1)
                        weigh(GROUPS + 1)
                        place_sums(pe, slot_sums, node_hot, GROUPS + 1)
            close_pass()

        with ExitStack() as stage:
            gained = stage.enter_context(nc.sbuf_tensor("gained", [PN, NT, D], f32))
            with nc.Block() as block:
                per = 16
                batches = [(b, min(per, NT - b)) for b in range(0, NT, per)]

                @block.tensor
                def _(pe):
                    for i, (b, n) in enumerate(batches):
                        if i >= 2:
                            pe.wait_ge(last_taken, i - 1)
                        for t in range(n):
                            last = pe.transpose(banks[i % 2][0:PN, t * D:(t + 1) * D],
                                                acc[0:D, b + t:b + t + (PN - 1) * NT + 1:NT], ident[0:D, 0:D])
                        last.then_inc(last_turned, 1)

                @block.vector
                def _(dve):
                    link = Chain(dve, last_chain)
                    for i, (b, n) in enumerate(batches):
                        dve.wait_ge(last_turned, i + 1)
                        dve.tensor_scalar(gained[:, b:b + n, :], banks[i % 2][0:PN, 0:n * D].rearrange("p (t d) -> p t d", d=D),
                                          0.0, None, ALU.max).then_inc(last_taken, 1)
                    dve.wait_ge(last_taken, len(batches))
                    link(dve.tensor_tensor(xb[:, :, :], xb[:, :, :], gained[:, :, :], ALU.add))

                @block.sync
                def _(sp):
                    sp.wait_ge(last_chain, 1)
                    sp.dma_start(out.rearrange("(p t) d -> p (t d)", t=NT), xb[:, :, :].rearrange("p t d -> p (t d)"))\
                      .then_inc(stored_out, 16)
                    sp.wait_ge(stored_out, 16)


_INS = ["x", "src", "dst", "edge_type_86", "node_vec1", "node_vec1_n2", "L1_gnn_weight", "L1_gnn_w_comp",
        "L1_gnn_self_loop_weight", "L1_gnn_A1_w", "L1_gnn_A1_b", "L1_gnn_A2_w", "L1_gnn_A2_b", "L1_gnn_rel_emb"]


def kernel(**inputs):
    import numpy as _np
    import concourse.bacc as _bacc
    from concourse import mybir as _mybir
    from concourse.bass_utils import run_bass_kernel_spmd as _run

    nc = _bacc.Bacc("TRN2", target_bir_lowering=False, num_devices=1)
    arrays, args = {}, []
    for name in _INS:
        a = _np.ascontiguousarray(inputs[name])
        arrays[f"in_{name}"] = a
        args.append(nc.dram_tensor(f"in_{name}", a.shape, _mybir.dt.from_np(a.dtype), kind="ExternalInput").ap())
    out = nc.dram_tensor("out_0", inputs["x"].shape, _mybir.dt.float32, kind="ExternalOutput").ap()
    gnn_kernel(nc, *args, out)
    r = _run(nc, [arrays], core_ids=[0])
    return r.results[0]["out_0"]
```
